# Optimizing a Trainium2 kernel written in Bass

```python
import numpy as np
import jax
import jax.numpy as jnp

def _softmax(x, axis=-1):
    return jax.nn.softmax(x, axis=axis)

def _gelu(x):
    return jax.nn.gelu(x, approximate=True)

def _silu(x):
    return jax.nn.silu(x)

def _sigmoid(x):
    return jax.nn.sigmoid(x)

def _layernorm(x, axis=-1, eps=1e-05):
    m = jnp.mean(x, axis=axis, keepdims=True)
    v = jnp.var(x, axis=axis, keepdims=True)
    return (x - m) / jnp.sqrt(v + eps)

def _scatter_add(tgt, idx, src, axis=0):
    return tgt.at[idx].add(src)

def _segment_sum(src, seg, n):
    return jax.ops.segment_sum(src, seg, n)
kernel_name = 'mk_prb_d1_jaxref_r8_678f8f'

def setup_inputs(seed: int=0):
    np.random.seed(seed)
    _w = jnp.asarray

    def _L0_attn_setup():
        import jax, jax.numpy as jnp
        import numpy as np
        B, T, H = (4, 512, 256)
        G_EPS = 0.5
        LN_EPS = 1e-05
        INIT_STD = 0.02

        def _g_log(x):
            return jnp.where(x >= 0, jnp.log(jax.nn.relu(x) + G_EPS), -jax.nn.softplus(-x))
        key = jax.random.key(seed)
        ks = jax.random.split(key, 4)
        return {'hidden_states': jax.random.normal(ks[0], (B, T, H), jnp.float32), 'W_z': jax.random.normal(ks[1], (H, H), jnp.float32) * INIT_STD, 'b_z': jnp.zeros((H,), jnp.float32), 'W_h': jax.random.normal(ks[2], (H, H), jnp.float32) * INIT_STD, 'b_h': jnp.zeros((H,), jnp.float32), 'ln_w': jnp.ones((H,), jnp.float32), 'ln_b': jnp.zeros((H,), jnp.float32), 'h0': jax.random.normal(ks[3], (H,), jnp.float32) * INIT_STD}
    _L0_attn_in = _L0_attn_setup()

    def _L0_ffn_setup():
        import jax, jax.numpy as jnp
        import numpy as np
        NUM_EXPERTS = 8
        TOP_K = 2
        HIDDEN = 256
        FFN = 704
        BATCH, SEQ = (2, 128)
        key = jax.random.key(seed)
        ks = jax.random.split(key, 5)
        scale = 0.02
        hidden_states = jax.random.normal(ks[0], (BATCH, SEQ, HIDDEN), dtype=jnp.float32)
        w_gate = jax.random.normal(ks[1], (NUM_EXPERTS, HIDDEN), dtype=jnp.float32) * scale
        w1 = jax.random.normal(ks[2], (NUM_EXPERTS, FFN, HIDDEN), dtype=jnp.float32) * scale
        w2 = jax.random.normal(ks[3], (NUM_EXPERTS, HIDDEN, FFN), dtype=jnp.float32) * scale
        w3 = jax.random.normal(ks[4], (NUM_EXPERTS, FFN, HIDDEN), dtype=jnp.float32) * scale
        return {'hidden_states': hidden_states, 'w_gate': w_gate, 'w1': w1, 'w2': w2, 'w3': w3}
    _L0_ffn_in = _L0_ffn_setup()
    _d = {'L0_attn_hidden_states': _L0_attn_in['hidden_states'], 'L0_attn_W_z': _L0_attn_in['W_z'], 'L0_attn_b_z': _L0_attn_in['b_z'], 'L0_attn_W_h': _L0_attn_in['W_h'], 'L0_attn_b_h': _L0_attn_in['b_h'], 'L0_attn_ln_w': _L0_attn_in['ln_w'], 'L0_attn_ln_b': _L0_attn_in['ln_b'], 'L0_attn_h0': _L0_attn_in['h0'], 'L0_ffn_w_gate': _L0_ffn_in['w_gate'], 'L0_ffn_w1': _L0_ffn_in['w1'], 'L0_ffn_w2': _L0_ffn_in['w2'], 'L0_ffn_w3': _L0_ffn_in['w3']}
    _x0 = _d['L0_attn_hidden_states']
    _d['L0_attn_hidden_states'] = jax.random.normal(jax.random.fold_in(jax.random.key(seed), 1), (2, 1024, 256), dtype=_x0.dtype)
    del _x0
    return _d

def reference(L0_attn_hidden_states, L0_attn_W_z, L0_attn_b_z, L0_attn_W_h, L0_attn_b_h, L0_attn_ln_w, L0_attn_ln_b, L0_attn_h0, L0_ffn_w_gate, L0_ffn_w1, L0_ffn_w2, L0_ffn_w3):

    def _L0_attn_ref(hidden_states, W_z, b_z, W_h, b_h, ln_w, ln_b, h0):
        import jax, jax.numpy as jnp
        import numpy as np
        B, T, H = (4, 512, 256)
        G_EPS = 0.5
        LN_EPS = 1e-05
        INIT_STD = 0.02

        def _g_log(x):
            return jnp.where(x >= 0, jnp.log(jax.nn.relu(x) + G_EPS), -jax.nn.softplus(-x))
        Bc, Tc, Hc = hidden_states.shape
        k = hidden_states @ W_z.T + b_z
        log_z = -jax.nn.softplus(-k)
        log_coeffs = -jax.nn.softplus(k)
        log_tilde_h = _g_log(hidden_states @ W_h.T + b_h)
        log_h0 = jnp.broadcast_to(_g_log(h0), (Bc, 1, Hc))
        log_values = jnp.concatenate([log_h0, log_z + log_tilde_h], axis=1)
        a_star = jnp.pad(jnp.cumsum(log_coeffs, axis=-1), ((0, 0), (1, 0), (0, 0)))
        log_h = a_star + jax.lax.cumlogsumexp(log_values - a_star, axis=1)
        log_h = (log_h - log_h.mean()) / jnp.std(log_h, ddof=1)
        h = jnp.exp(log_h)[:, 1:, :]
        x = h + hidden_states
        mu = x.mean(axis=-1, keepdims=True)
        var = x.var(axis=-1, keepdims=True)
        return (x - mu) * jax.lax.rsqrt(var + LN_EPS) * ln_w + ln_b

    def _L0_ffn_ref(hidden_states, w_gate, w1, w2, w3):
        import jax, jax.numpy as jnp
        import numpy as np
        NUM_EXPERTS = 8
        TOP_K = 2
        HIDDEN = 256
        FFN = 704
        BATCH, SEQ = (2, 128)
        B, S, D = hidden_states.shape
        x = hidden_states.reshape(-1, D)
        router_logits = x @ w_gate.T
        routing_weights = jax.nn.softmax(router_logits.astype(jnp.float32), axis=-1)
        routing_weights, selected_experts = jax.lax.top_k(routing_weights, TOP_K)
        routing_weights = routing_weights / jnp.sum(routing_weights, axis=-1, keepdims=True)
        routing_weights = routing_weights.astype(x.dtype)
        out = jnp.zeros_like(x)
        for e in range(NUM_EXPERTS):
            expert_weight = jnp.sum(routing_weights * (selected_experts == e), axis=-1, keepdims=True)
            h = jax.nn.silu(x @ w1[e].T) * (x @ w3[e].T)
            out = out + h @ w2[e].T * expert_weight
        return out.reshape(B, S, D)
    x = L0_attn_hidden_states
    xn = _layernorm(x, axis=-1)
    x = x + _L0_attn_ref(xn, L0_attn_W_z, L0_attn_b_z, L0_attn_W_h, L0_attn_b_h, L0_attn_ln_w, L0_attn_ln_b, L0_attn_h0) + _L0_ffn_ref(xn, L0_ffn_w_gate, L0_ffn_w1, L0_ffn_w2, L0_ffn_w3)
    return x

_drawn_inputs = setup_inputs


def setup_inputs(seed=0):
    import zlib

    import numpy as np

    out = dict(_drawn_inputs(seed))
    spreads = {'L0_attn_b_z': (0.0, 1.18),
     'L0_attn_b_h': (0.0, 0.939),
     'L0_attn_ln_w': (1.0, 0.2),
     'L0_attn_ln_b': (0.0, 0.389)}
    factors = {'L0_attn_h0': 64.0,
     'L0_ffn_w_gate': 6.286,
     'L0_ffn_w1': 5.52,
     'L0_ffn_w2': 5.451,
     'L0_ffn_w3': 5.452,
     'L0_attn_W_h': 6.592}
    for name, (base, spread) in spreads.items():
        noise = np.random.default_rng([zlib.crc32(name.encode()), seed]).standard_normal(out[name].shape)
        drawn = base * np.exp(spread * noise) if base else spread * noise
        out[name] = jnp.asarray(drawn.astype(out[name].dtype))
    for name, factor in factors.items():
        out[name] = (out[name] * factor).astype(out[name].dtype)
    return out
```

```python
import concourse.bass as bass
from concourse import mybir
from contextlib import ExitStack

P = 128
B, T, D = 2, 1024, 256
NTOK = B * T
NT = NTOK // P
Q = D // P
E, F = 8, 704
NTILES = (2 * NTOK + E * (P - 1)) // P
NCOL = NTILES + 3
FULL = F // P
HC = FULL + 1
TAIL = F - FULL * P
W13 = Q * 2 * F
WMAIN = W13 + FULL * D
WALL = WMAIN + D
CH = 512
NCH = NTOK // CH
LN_EPS = 1e-5
NSTAT = B * (T + 1) * D
SCRATCH = 2 * NTOK
UP_PIECES = [(0, 512), (512, 1024), (1024, 1408)]
BIG = 3.0e38


def build_program(nc, x, wzh, bias, h0, ln_wb, wg, w_main, w_tail, out, xn_dram, y_dram):
    fp32, f32r, i32 = mybir.dt.float32, mybir.dt.float32r, mybir.dt.int32
    u32, bf16 = mybir.dt.uint32, mybir.dt.bfloat16
    ALU, ACT, AX = mybir.AluOpType, mybir.ActivationFunctionType, mybir.AxisListType
    ds = bass.ds
    ctx = ExitStack()
    with ctx:
        def sb(name, shape, dt=fp32):
            return ctx.enter_context(nc.sbuf_tensor(name, shape, dt))

        def sem(name):
            return ctx.enter_context(nc.semaphore(name))

        xn = sb("xn", [P, NT, D])
        xnT_M = sb("xnT_M", [P, 4 * (T + 1)])
        xnT = xnT_M[:, 0:Q * NTOK].rearrange("p (q n) -> p q n", q=Q)
        M = xnT_M[:, :].rearrange("p (g t) -> p g t", g=4)
        U = sb("U", [P, 2 * NTOK])
        Ug = U[:, :].rearrange("p (g t) -> p g t", g=4)
        A = sb("A", [P, 2 * NTOK])
        Ag = A[:, :].rearrange("p (g t) -> p g t", g=4)
        wbuf = sb("wbuf", [P, 2, 2, WALL], f32r)
        raw = sb("raw", [P, WALL])
        tmp = sb("tmp", [P, 5, Q * CH])
        kb, l1, l3, nn, l2 = (tmp[:, n, :] for n in range(5))
        tflat = tmp[:, :, :].rearrange("p a n -> p (a n)")
        g_h = tflat[:, 0:F]
        sl = tflat[:, F:2 * F]
        Dm = tmp[:, 2, :]
        Sm = tmp[:, 3, :]
        hst = sb("hst", [P, Q, 2 * P])
        eps = sb("eps", [P, 1])
        hT = sb("hT", [P, 2, HC * P], f32r)
        xT = sb("xT", [P, 2, 2, D], f32r)
        onehot_tile = hT[:, :, :].rearrange("p a n -> p (a n)")[:, 0:2 * NT * NCOL]
        onehot_pos = xT[:, :, :, :].rearrange("p a b n -> p a (b n)")
        xg = sb("xg", [P, 2, D])
        ysb = sb("ysb", [P, 2, D])
        xre = sb("xre", [P, 2, D])
        wzh_sb = sb("wzh_sb", [P, Q, 2, D])
        wg_sb = sb("wg_sb", [P, Q, E])
        bias_sb = sb("bias_sb", [P, 2, Q])
        h0_sb = sb("h0_sb", [P, Q])
        lnwb = sb("lnwb", [P, 2, D])
        ident = sb("ident", [P, P])
        tri = sb("tri", [P, P])
        ones = sb("ones", [P, P])
        tri_b = sb("tri_b", [P, P], bf16)
        ones_b = sb("ones_b", [P, P], bf16)
        pick_b = sb("pick_b", [P, NT * E], bf16)
        iota_c = sb("iota_c", [P, P])
        bst = sb("bst", [P, NT, 6])
        mv = sb("mv", [P, NT, 2])
        rstd = sb("rstd", [P, NT])
        w12 = sb("w12", [P, 2, NT])
        slot_i = sb("slot_i", [P, 3, 2 * NT], i32)
        gcol = sb("gcol", [P, 2], u32)
        scol = sb("scol", [P, 2], u32)
        gidx = sb("gidx", [P, NCOL], u32)
        sidx = sb("sidx", [P, NCOL], u32)
        eid = sb("eid", [P, NCOL], i32)
        first = sb("first", [P, NCOL], i32)
        u0 = sb("u0", [P, 4])
        u0t = sb("u0t", [P, 6, Q])
        gst = sb("gst", [P, 8, 6])
        gs = sb("gs", [P, 16])
        st3 = sb("st3", [P, 2, 6])
        mv3 = sb("mv3", [P, 2, 2])
        rtmp = sb("rtmp", [P, 2, D])
        std = sb("std", [P, NT])
        at = [0]

        def ut(cols):
            at[0] += cols
            return U[:, at[0] - cols:at[0]]
        logit = ut(NT * E)
        t_a, t_b, hot1, hot2, pick, slots = (ut(NT * E) for _ in range(6))
        tot = ut(E * NT)
        cum = ut(E * NT)
        keep = ut(E * NT)
        m12 = ut(2 * NT)
        idx8 = ut(NT)
        slot_f, pos_f, tile_f, id_f = (ut(2 * NT) for _ in range(4))
        cnt, ntile, tend, tstart, one8 = (ut(E) for _ in range(5))
        thr = ut(E * NT)
        dtab, dpad, dtok = (ut(NCOL) for _ in range(3))
        pad_row = ut(NCOL)
        cmp8 = ut(NCOL * E)
        eid_f = ut(NCOL)

        PS = ctx.enter_context(nc.psum_tensor("PS", [P, 8 * 512], fp32))
        up_ps = PS[:, 0:2 * F]
        hT_ps = PS[:, 3 * 512:3 * 512 + HC * P]
        xT_ps = PS[:, 5 * 512:5 * 512 + D]
        y_ps = PS[:, 6 * 512:6 * 512 + D]
        tr_ps = PS[:, 7 * 512:8 * 512]
        k_ps = PS[:, 0:2 * CH]
        yh_ps = PS[:, 2 * CH:4 * CH]
        cum_ps = PS[:, 4 * CH:6 * CH]
        rank_ps = PS[:, 6 * 512:6 * 512 + NT * E]
        tot_ps = PS[:, 6 * 512 + 128:6 * 512 + 128 + NT * E]
        table_ps = PS[:, 6 * 512 + 256:6 * 512 + 256 + NCOL]
        stat_ps = PS[:, 7 * 512:7 * 512 + 4]
        logit_ps = PS[:, 7 * 512:7 * 512 + NT * E]

        s_x = [sem(f"x_loaded{g}") for g in range(4)]
        s_small = sem("small_inputs_loaded")
        s_small2 = sem("more_inputs_loaded")
        s_raw = sem("expert_loaded")
        s_const = sem("constants_made")
        s_pool = sem("pool_steps")
        s_dve = sem("dve_steps")
        s_act = sem("act_steps")
        s_xn = sem("xn_group_ready")
        s_xnd = sem("xn_stored")
        s_xtr = sem("xn_transposed")
        s_xnT = sem("xnT_ready")
        s_lg = sem("logits_done")
        s_pick = sem("picks_ready")
        s_rank = sem("ranks_done")
        s_pos = sem("onehots_ready")
        s_posu = sem("onehots_used")
        s_idx = sem("tables_ready")
        s_zin = sem("gap_ready")
        s_zex = sem("gap_exp_done")
        s_u0a = sem("u0_exp_done")
        s_u0b = sem("u0_logs_done")
        s_u0i = sem("u0_inputs_ready")
        s_k = sem("k_projected")
        s_kb = sem("kb_ready")
        s_e = sem("act_chain")
        s_l1 = sem("l1_ready")
        s_n = sem("n_ready")
        s_l3 = sem("l3_ready")
        s_l2 = sem("l2_ready")
        s_c = sem("c_ready")
        s_cum = sem("cumsum_done")
        s_acp = sem("a_star_copied")
        s_u1 = sem("l3_minus_l2_ready")
        s_u2 = sem("k_minus_c_ready")
        s_ua = sem("u_partial_sums")
        s_U = sem("u_ready")
        s_hi = sem("expert_hi_ready")
        s_w = sem("expert_ready")
        s_ga = sem("even_tile_gathered")
        s_gb = sem("odd_tile_gathered")
        s_gc = sem("gather_column_ready")
        s_sc = sem("scatter_column_ready")
        s_xt = sem("x_tile_transposed")
        s_xhi = sem("x_hi_ready")
        s_xlo = sem("x_lo_ready")
        s_up = sem("up_done")
        s_silu = sem("silu_ready")
        s_g = sem("gated_ready")
        s_ht = sem("gated_transposed")
        s_hhi = sem("h_hi_ready")
        s_hlo = sem("h_lo_ready")
        s_dn = sem("down_done")
        s_y = sem("y_copied")
        s_sa = sem("even_tile_scattered")
        s_sb = sem("odd_tile_scattered")
        s_M = sem("running_max_ready")
        s_D = sem("max_steps_ready")
        s_Em = sem("u_minus_max_ready")
        s_De = sem("decay_ready")
        s_Ee = sem("increment_ready")
        s_S = sem("scan_ready")
        s_lS = sem("log_scan_ready")
        s_L = sem("log_plus_max_ready")
        s_lh = sem("log_h_ready")
        s_mean_in = sem("sums_ready")
        s_mean = sem("mean_summed")
        s_var_in = sem("squares_ready")
        s_var = sem("squares_summed")
        s_norm = sem("norm_ready")
        s_xre = sem("x_loaded_again")
        s_h = sem("h_ready")
        s_htr = sem("h_transposed")
        s_p1 = sem("stats_steps")
        s_p2 = sem("last_norm_steps")
        s_var0 = sem("group_variance_ready")
        s_std0 = sem("group_deviation_ready")
        s_std = sem("log_h_deviation_ready")
        s_std3 = sem("row_deviations_ready")
        s_yl = [sem(f"y_loaded{g}") for g in range(4)]
        s_fin = sem("result_ready")
        s_out = sem("result_stored")

        block = ctx.enter_context(nc.Block())

        def hold(eng, s, value):
            eng.wait_ge(s, value)
            eng.nop(nofuse=True)

        def wslot(e, part, a, b):
            return wbuf[:, ds(e % 2, 1), part, a:b].rearrange("p s n -> p (s n)")

        @block.sync
        def _(sp):
            for g in range(4):
                sp.dma_start(xn[:, 4 * g:4 * g + 4, :],
                             x[512 * g:512 * (g + 1), :].rearrange("(t p) d -> p t d", p=P)).then_inc(s_x[g], 16)
            sp.dma_start(raw[:, 0:WMAIN], w_main[0]).then_inc(s_raw, 16)
            sp.dma_start(raw[P - TAIL:P, WMAIN:WALL], w_tail[0]).then_inc(s_raw, 16)
            for g in range(4):
                sp.wait_ge(s_xn, g + 1)
                sp.dma_start(xn_dram[512 * g:512 * (g + 1), :].rearrange("(t p) d -> p t d", p=P),
                             xn[:, 4 * g:4 * g + 4, :]).then_inc(s_xnd, 16)
            with sp.Fori(1, E) as e:
                sp.wait_ge(s_w, e)
                sp.dma_start(raw[:, 0:WMAIN],
                             w_main[ds(e, 1)].rearrange("a p n -> (a p) n")).then_inc(s_raw, 16)
                sp.dma_start(raw[P - TAIL:P, WMAIN:WALL],
                             w_tail[ds(e, 1)].rearrange("a p n -> (a p) n")).then_inc(s_raw, 16)
            sp.wait_ge(s_sa, 16 * ((NTILES + 1) // 2 + 1))
            sp.wait_ge(s_sb, 16 * (NTILES // 2 + 1))
            for g in range(4):
                for k, buf in ((0, U), (1, A)):
                    sp.dma_start(buf[:, 1024 * g:1024 * (g + 1)].rearrange("p (t d) -> p t d", d=D),
                                 y_dram[k * NTOK + 512 * g:k * NTOK + 512 * (g + 1), :]
                                 .rearrange("(t p) d -> p t d", p=P)).then_inc(s_yl[g], 16)
            for g in range(4):
                sp.wait_ge(s_fin, g + 1)
                sp.dma_start(out[512 * g:512 * (g + 1), :].rearrange("(t p) d -> p t d", p=P),
                             xn[:, 4 * g:4 * g + 4, :]).then_inc(s_out, 16)
            sp.wait_ge(s_out, 64)

        @block.gpsimd
        def _(pool):
            n = [0]

            def step(ins):
                n[0] += 1
                ins.then_inc(s_pool, 1)
                pool.wait_ge(s_pool, n[0])
            pool.memset(ident[:, :], 0.0).then_inc(s_const, 1)
            pool.memset(ones[:, :], 1.0).then_inc(s_const, 1)
            pool.memset(tri[:, :], 1.0).then_inc(s_const, 1)
            pool.memset(ones_b[:, :], 1.0).then_inc(s_const, 1)
            pool.memset(tri_b[:, :], 1.0).then_inc(s_const, 1)
            pool.memset(raw[0:P - TAIL, WMAIN:WALL], 0.0).then_inc(s_const, 1)
            pool.wait_ge(s_const, 6)
            pool.affine_select(out=ident[:, :], in_=ident[:, :], compare_op=ALU.not_equal, fill=1.0, base=0,
                               pattern=[[-1, P]], channel_multiplier=1).then_inc(s_const, 1)
            pool.affine_select(out=tri[:, :], in_=tri[:, :], compare_op=ALU.is_ge, fill=0.0, base=0,
                               pattern=[[1, P]], channel_multiplier=-1).then_inc(s_const, 1)
            pool.affine_select(out=tri_b[:, :], in_=tri_b[:, :], compare_op=ALU.is_gt, fill=0.0, base=0,
                               pattern=[[1, P]], channel_multiplier=-1).then_inc(s_const, 1)
            pool.iota(iota_c[:, :], [[1, P]], base=0, channel_multiplier=0,
                      allow_small_or_imprecise_dtypes=True).then_inc(s_const, 1)
            pool.iota(id_f.rearrange("p (k t) -> p k t", k=2), [[NTOK, 2], [P, NT]], base=1, channel_multiplier=1,
                      allow_small_or_imprecise_dtypes=True).then_inc(s_const, 1)
            pool.iota(pad_row.rearrange("p (c u) -> p c u", u=2), [[0, NCOL // 2], [P, 2]], base=SCRATCH + 1,
                      channel_multiplier=1, allow_small_or_imprecise_dtypes=True).then_inc(s_const, 1)
            pool.memset(eps[:, :], LN_EPS).then_inc(s_const, 1)
            pool.memset(ysb[:, :, :], 0.0).then_inc(s_const, 1)
            pool.wait_ge(s_const, 14)
            pool.dma_start(y_dram[SCRATCH + 2 * P:SCRATCH + 3 * P, :], ysb[:, 0, :]).then_inc(s_sa, 16)
            pool.dma_start(y_dram[SCRATCH + 3 * P:SCRATCH + 4 * P, :], ysb[:, 1, :]).then_inc(s_sb, 16)
            pool.wait_ge(s_raw, 32)
            pool.tensor_copy(wbuf[:, 0, 0, :], raw[:, :]).then_inc(s_hi, 1)
            pool.wait_ge(s_hi, 1)
            pool.tensor_tensor(wbuf[:, 0, 1, :], raw[:, :], wbuf[:, 0, 0, :].bitcast(fp32),
                               ALU.subtract).then_inc(s_w, 1)
            pool.wait_ge(s_idx, 1)
            pool.wait_ge(s_xnd, 64)

            def gather(j, slot, s):
                pool.tensor_copy(gcol[:, slot:slot + 1], gidx[:, ds(j, 1)]).then_inc(s_gc, 1)
                hold(pool, s_gc, j + 1)
                pool.indirect_dma_start(xg[:, slot, :], None, xn_dram,
                                        bass.IndirectOffsetOnAxis(gcol[:, slot:slot + 1], 0)).then_inc(s, 16)

            def scatter(j, slot, s):
                pool.wait_ge(s_y, j + 2)
                pool.tensor_copy(scol[:, slot:slot + 1], sidx[:, ds(j, 1)]).then_inc(s_sc, 1)
                hold(pool, s_sc, j + 1)
                pool.indirect_dma_start(y_dram, bass.IndirectOffsetOnAxis(scol[:, slot:slot + 1], 0),
                                        ysb[:, slot, :], None).then_inc(s, 16)

            def split_lo(e):
                hold(pool, s_hi, e + 2)
                pool.tensor_tensor(wslot(e + 1, 1, 0, WALL), raw[:, :], wslot(e + 1, 0, 0, WALL).bitcast(fp32),
                                   ALU.subtract).then_inc(s_w, 1)
            gather(0, 0, s_ga)
            gather(1, 1, s_gb)
            with pool.Fori(0, NCH) as c:
                pool.wait_ge(s_l3, c + 1)
                hold(pool, s_l2, c + 1)
                pool.tensor_tensor(l3, l3, l2, ALU.subtract).then_inc(s_u1, 1)
                hold(pool, s_c, c + 1)
                pool.tensor_tensor(kb, kb, l1, ALU.subtract).then_inc(s_u2, 1)
            pool.wait_ge(s_xt, 1)
            gather(2, 0, s_ga)
            pool.wait_ge(s_hi, 2)
            pool.tensor_tensor(wbuf[:, 1, 1, :], raw[:, :], wbuf[:, 1, 0, :].bitcast(fp32),
                               ALU.subtract).then_inc(s_w, 1)

            def tile_step(j, u, hook=None):
                odd = u == 0
                pool.wait_ge(s_xt, j + 1)
                gather(j + 2, 1 if odd else 0, s_gb if odd else s_ga)
                if hook:
                    hook()
                scatter(j - 1, 0 if odd else 1, s_sa if odd else s_sb)
                starts = pool.value_load(first[0:1, ds(j, 1)], min_val=0, max_val=1)
                e = pool.value_load(eid[0:1, ds(j, 1)], min_val=0, max_val=E - 1)
                with pool.If(starts > 0):
                    split_lo(e)

            def em(i):
                def run():
                    hold(pool, s_M, i + 1)
                    pool.tensor_tensor(Ug[:, ds(i, 1), :], Ug[:, ds(i, 1), :], M[:, ds(i, 1), 1:T + 1],
                                       ALU.subtract).then_inc(s_Em, 1)
                return run

            def logh(i):
                def run():
                    hold(pool, s_lS, i + 1)
                    pool.tensor_tensor(Sm.rearrange("p (a t) -> p a t", a=1), M[:, ds(i, 1), 1:T + 1],
                                       Sm.rearrange("p (a t) -> p a t", a=1), ALU.add).then_inc(s_L, 1)
                    hold(pool, s_L, i + 1)
                    pool.tensor_tensor(Ag[:, ds(i, 1), :], Sm.rearrange("p (a t) -> p a t", a=1),
                                       Ag[:, ds(i, 1), :], ALU.subtract).then_inc(s_lh, 1)
                return run

            with pool.Fori(0, 4) as i:
                tile_step(2 * i + 1, 0, em(i))
                tile_step(2 * i + 2, 1, logh(i))
            with pool.Fori(4, (NTILES - 1) // 2) as i:
                tile_step(2 * i + 1, 0)
                tile_step(2 * i + 2, 1)
            scatter(NTILES - 1, 0, s_sa)
            pool.wait_ge(s_ga, 16 * 21)
            pool.wait_ge(s_gb, 16 * 20)

        @block.scalar
        def _(act):
            n = [0]
            for dst, src in ((wzh_sb, wzh), (wg_sb, wg)):
                act.dma_start(dst[:, :, :, :] if dst is wzh_sb else dst[:, :, :], src).then_inc(s_small, 16)
            act.dma_start(bias_sb[:, :, :], bias).then_inc(s_small2, 16)
            act.dma_start(h0_sb[:, :], h0).then_inc(s_small2, 16)
            act.dma_start(lnwb[:, :, :], ln_wb).then_inc(s_small2, 16)
            act.wait_ge(s_const, 14)
            for g in range(4):
                act.wait_ge(s_var0, g + 1)
                act.activation(std[:, 4 * g:4 * g + 4], mv[:, 4 * g:4 * g + 4, 1], ACT.Sqrt,
                               bias=eps[:, :]).then_inc(s_std0, 1)
            for m in range(NT // 2):
                act.wait_ge(s_xtr, m + 1)
                act.activation(xnT[:, :, 2 * P * m:2 * P * (m + 1)].rearrange("p q (t n) -> p t q n", t=2),
                               PS[:, (4 + m % 2) * 512:(5 + m % 2) * 512].rearrange("p (t q n) -> p t q n", t=2, q=Q),
                               ACT.Copy).then_inc(s_xnT, 1)
            act.wait_ge(s_u0i, 2)
            act.activation(u0t[:, 2, :], u0t[:, 0, :], ACT.Exp).then_inc(s_u0a, 1)
            act.activation(u0t[:, 3, :], u0t[:, 1, :], ACT.Ln, scale=2.0, bias=1.0).then_inc(s_u0b, 1)
            act.wait_ge(s_u0a, 1)
            act.activation(u0t[:, 4, :], u0t[:, 2, :], ACT.Ln, bias=1.0).then_inc(s_u0b, 1)
            act.wait_ge(s_zin, 1)
            act.activation(w12[:, 1, :], w12[:, 0, :], ACT.Exp).then_inc(s_zex, 1)
            act.wait_ge(s_small2, 48)

            def chunk(c):
                act.wait_ge(s_k, c + 1)
                act.wait_ge(s_U, c + 1)
                for q in range(Q):
                    act.activation(kb[:, q * CH:(q + 1) * CH], k_ps[:, q * CH:(q + 1) * CH], ACT.Identity,
                                   bias=bias_sb[:, 0, q:q + 1]).then_inc(s_kb, 1)
                for q in range(Q):
                    act.activation(l3[:, q * CH:(q + 1) * CH], yh_ps[:, q * CH:(q + 1) * CH], ACT.Relu,
                                   bias=bias_sb[:, 1, q:q + 1]).then_inc(s_e, 1)
                act.wait_ge(s_kb, 2 * c + 2)
                act.activation(l1, kb, ACT.Abs).then_inc(s_e, 1)
                act.wait_ge(s_e, 5 * c + 3)
                act.activation(l1, l1, ACT.Exp, scale=-1.0).then_inc(s_e, 1)
                act.wait_ge(s_e, 5 * c + 4)
                act.activation(l1, l1, ACT.Ln, bias=1.0).then_inc(s_l1, 1)
                act.activation(l3, l3, ACT.Ln, scale=2.0, bias=1.0).then_inc(s_l3, 1)
                act.wait_ge(s_n, 2 * c + 2)
                act.activation(l2, nn, ACT.Exp).then_inc(s_e, 1)
                act.wait_ge(s_e, 5 * c + 5)
                act.activation(l2, l2, ACT.Ln, bias=1.0).then_inc(s_l2, 1)
                act.wait_ge(s_cum, c + 1)
                act.activation(A[:, :].rearrange("p (q n) -> p q n", q=Q)[:, :, ds(c * CH, CH)],
                               cum_ps.rearrange("p (q n) -> p q n", q=Q), ACT.Copy).then_inc(s_acp, 1)
            with act.Fori(0, NCH) as c:
                chunk(c)

            def x_hi(j, slot):
                act.wait_ge(s_xt, j + 1)
                act.activation(xT[:, slot, 0, :], xT_ps, ACT.Copy).then_inc(s_xhi, 1)

            def h_hi(j):
                act.wait_ge(s_ht, j + 1)
                act.wait_ge(s_dn, j + 0)
                act.activation(hT[:, 0, :], hT_ps, ACT.Copy).then_inc(s_hhi, 1)

            def silu(j):
                act.wait_ge(s_up, j + 1)
                act.activation(sl, up_ps[:, 0:F], ACT.Silu).then_inc(s_silu, 1)

            x_hi(0, 0)
            act.wait_ge(s_U, NCH + 1)
            silu(0)
            x_hi(1, 1)
            act.wait_ge(s_ht, 1)
            act.activation(hT[:, 0, :], hT_ps, ACT.Copy).then_inc(s_hhi, 1)

            def tile_step(j, u, ysem, yval, before=None, after=None):
                silu(j)
                x_hi(j + 1, 0 if u == 0 else 1)
                if before:
                    before()
                act.wait_ge(s_dn, j)
                act.wait_ge(ysem, yval)
                act.activation(ysb[:, 0 if u == 0 else 1, :], y_ps, ACT.Copy).then_inc(s_y, 1)
                h_hi(j)
                if after:
                    after()

            def pair(i, hooks=(None, None, None, None)):
                tile_step(2 * i + 1, 0, s_sa, 16 * i + 16, hooks[0], hooks[1])
                tile_step(2 * i + 2, 1, s_sb, 16 * i + 16, hooks[2], hooks[3])

            def exps(i):
                def run():
                    act.wait_ge(s_D, i + 1)
                    act.activation(Dm, Dm, ACT.Exp).then_inc(s_De, 1)
                    act.wait_ge(s_Em, i + 1)
                    act.activation(Ug[:, ds(i, 1), :], Ug[:, ds(i, 1), :], ACT.Exp).then_inc(s_Ee, 1)
                return run

            def logs(i):
                def run():
                    act.wait_ge(s_S, i + 1)
                    act.activation(Sm, Sm, ACT.Ln).then_inc(s_lS, 1)
                return run

            def h_exp(m):
                def run():
                    act.wait_ge(s_htr, m + 1)
                    act.activation(hst[:, :, :], A[:, :].rearrange("p (q n) -> p q n", q=Q)[:, :, ds(m * 2 * P, 2 * P)],
                                   ACT.Exp, scale=gs[:, 8:9], bias=gs[:, 9:10]).then_inc(s_h, 1)
                return run

            def x_again(m):
                def run():
                    act.wait_ge(s_p2, 4 * m + 1)
                    act.dma_start(xre[:, :, :], x[ds(m * 2 * P, 2 * P), :].rearrange("(t p) d -> p t d", p=P)
                                  ).then_inc(s_xre, 16)
                return run
            with act.Fori(0, 4) as i:
                pair(i, (None, exps(i), None, logs(i)))
            pair(4)
            tile_step(11, 0, s_sa, 16 * 6)
            act.wait_ge(s_var, 1)
            act.activation(gs[:, 15:16], stat_ps[:, 2:3], ACT.Sqrt, scale=1.0 / (NSTAT - 1)).then_inc(s_std, 1)
            tile_step(12, 1, s_sb, 16 * 6)
            act.wait_ge(s_norm, 1)
            with act.Fori(6, 10) as i:
                pair(i, (h_exp(2 * i - 12), None, h_exp(2 * i - 11), None))
            act.wait_ge(s_p1, 4 * NT // 2 + 1)
            act.activation(std[:, :], mv[:, :, 1], ACT.Sqrt, bias=eps[:, :]).then_inc(s_std3, 1)
            with act.Fori(10, 14) as i:
                pair(i, (x_again(2 * i - 20), None, x_again(2 * i - 19), None))
            with act.Fori(14, (NTILES - 1) // 2) as i:
                pair(i)
            act.wait_ge(s_dn, NTILES)
            act.wait_ge(s_sa, 16 * 19 + 16)
            act.activation(ysb[:, 0, :], y_ps, ACT.Copy).then_inc(s_y, 1)

        @block.vector
        def _(dve):
            n = [0]

            def step(ins):
                n[0] += 1
                ins.then_inc(s_dve, 1)
                dve.wait_ge(s_dve, n[0])

            dve.sem_inc(s_U, 1)
            dve.sem_inc(s_acp, 1)
            dve.sem_inc(s_y, 1)
            dve.sem_inc(s_htr, 1)
            dve.sem_inc(s_p1, 1)
            dve.sem_inc(s_p2, 1)
            dve.memset(one8, 1.0)
            dve.memset(keep.rearrange("p (e t) -> p e t", e=E)[:, :, 1:NT], 1.0)
            dve.memset(keep.rearrange("p (e t) -> p e t", e=E)[:, :, 0:1], 0.0)
            dve.wait_ge(s_small2, 48)
            dve.tensor_scalar(u0t[:, 0, :], h0_sb[:, :], 0.0, None, ALU.min).then_inc(s_u0i, 1)
            dve.tensor_scalar(u0t[:, 1, :], h0_sb[:, :], 0.0, None, ALU.max).then_inc(s_u0i, 1)
            for g in range(4):
                dve.wait_ge(s_x[g], 16)
                for t in range(4 * g, 4 * g + 4):
                    ins = dve.bn_stats(bst[:, t, :], xn[:, t, :])
                step(ins)
                for t in range(4 * g, 4 * g + 4):
                    ins = dve.bn_aggr(mv[:, t, :], bst[:, t, :])
                ins.then_inc(s_var0, 1)
                dve.wait_ge(s_std0, g + 1)
                step(dve.reciprocal(rstd[:, 4 * g:4 * g + 4], std[:, 4 * g:4 * g + 4]))
                for t in range(4 * g, 4 * g + 4):
                    ins = dve.tensor_scalar(xn[:, t, :], xn[:, t, :], mv[:, t, 0:1], rstd[:, t:t + 1],
                                            ALU.subtract, ALU.mult)
                ins.then_inc(s_xn, 1)
            dve.wait_ge(s_lg, 1)

            def te(v):
                return v.rearrange("p (t e) -> p t e", e=E)

            def over_e(v):
                return v.rearrange("p (t a) -> p t a", a=1).to_broadcast([P, NT, E])
            ramp = iota_c[:, 0:E].rearrange("p (a e) -> p a e", a=1).to_broadcast([P, NT, E])
            step(dve.tensor_copy(logit, logit_ps))
            m1, m2 = m12[:, 0:NT], m12[:, NT:2 * NT]
            for mx, src, hot in ((m1, logit, hot1), (m2, t_b, hot2)):
                step(dve.tensor_reduce(mx, te(src), AX.X, ALU.max))
                step(dve.tensor_tensor(te(t_a), te(src), over_e(mx), ALU.is_equal))
                step(dve.scalar_tensor_tensor(te(t_a), ramp, float(P), te(t_a), ALU.subtract, ALU.mult))
                step(dve.tensor_reduce(idx8, te(t_a), AX.X, ALU.min))
                step(dve.scalar_tensor_tensor(te(hot), ramp, float(P), over_e(idx8), ALU.subtract, ALU.is_equal))
                if hot is hot1:
                    step(dve.scalar_tensor_tensor(t_b, hot1, -BIG, logit, ALU.mult, ALU.add))
            dve.tensor_tensor(w12[:, 0, :], m2, m1, ALU.subtract).then_inc(s_zin, 1)
            step(dve.tensor_tensor(pick, hot1, hot2, ALU.add))
            dve.tensor_copy(pick_b[:, :], pick).then_inc(s_pick, 1)
            dve.wait_ge(s_zex, 1)
            step(dve.tensor_scalar(w12[:, 0, :], w12[:, 1, :], 1.0, None, ALU.add))
            step(dve.reciprocal(w12[:, 0, :], w12[:, 0, :]))
            step(dve.tensor_tensor(w12[:, 1, :], w12[:, 1, :], w12[:, 0, :], ALU.mult))
            dve.wait_ge(s_rank, 1)
            et = "p (e t) -> p e t"
            step(dve.tensor_copy(tot.rearrange(et, e=E), tot_ps.rearrange("p (t e) -> p e t", e=E)))
            step(dve.tensor_tensor_scan(cum, keep, tot, 0.0, ALU.mult, ALU.add))
            step(dve.tensor_copy(cnt, cum.rearrange(et, e=E)[:, :, NT - 1]))
            step(dve.tensor_scalar(eid_f[:, 0:NT], iota_c[:, 0:NT], float(P), None, ALU.mult))
            step(dve.tensor_tensor(thr.rearrange(et, e=E), cnt.rearrange("p (e a) -> p e a", a=1).to_broadcast([P, E, NT]),
                                   eid_f[:, 0:NT].rearrange("p (a t) -> p a t", a=1).to_broadcast([P, E, NT]), ALU.is_gt))
            step(dve.tensor_reduce(ntile, thr.rearrange(et, e=E), AX.X, ALU.add))
            step(dve.tensor_scalar(ntile, ntile, 1.0, None, ALU.max))
            step(dve.tensor_tensor_scan(tend, one8, ntile, 0.0, ALU.mult, ALU.add))
            step(dve.tensor_tensor(tstart, tend, ntile, ALU.subtract))
            step(dve.tensor_tensor(cum, cum, tot, ALU.subtract))
            step(dve.scalar_tensor_tensor(cum.rearrange(et, e=E), tstart.rearrange("p (e a) -> p e a", a=1)
                                          .to_broadcast([P, E, NT]), float(P), cum.rearrange(et, e=E), ALU.mult, ALU.add))
            step(dve.tensor_tensor(te(slots), cum.rearrange("p (e t) -> p t e", e=E), te(rank_ps), ALU.add))
            for k, hot in ((0, hot1), (1, hot2)):
                step(dve.tensor_tensor(t_a, hot, slots, ALU.mult))
                step(dve.tensor_reduce(slot_f[:, k * NT:(k + 1) * NT], te(t_a), AX.X, ALU.add))
            step(dve.tensor_copy(slot_i[:, 0, :], slot_f))
            step(dve.tensor_scalar(slot_i[:, 1, :], slot_i[:, 0, :], P - 1, None, ALU.bitwise_and))
            step(dve.tensor_scalar(slot_i[:, 2, :], slot_i[:, 0, :], 7, None, ALU.logical_shift_right))
            step(dve.tensor_copy(pos_f, slot_i[:, 1, :]))
            step(dve.tensor_copy(tile_f, slot_i[:, 2, :]))
            oh = onehot_tile.rearrange("p (s c) -> p s c", c=NCOL)
            step(dve.tensor_tensor(oh, iota_c[:, 0:NCOL].rearrange("p (a c) -> p a c", a=1).to_broadcast([P, 2 * NT, NCOL]),
                                   tile_f.rearrange("p (s a) -> p s a", a=1).to_broadcast([P, 2 * NT, NCOL]), ALU.is_equal))
            step(dve.tensor_tensor(oh, oh.bitcast(fp32), id_f.rearrange("p (s a) -> p s a", a=1)
                                   .to_broadcast([P, 2 * NT, NCOL]), ALU.mult))
            for m in range(2 * NT // 4):
                if m >= 2:
                    dve.wait_ge(s_posu, m - 1)
                dve.tensor_tensor(onehot_pos[:, m % 2, :].rearrange("p (s c) -> p s c", c=P),
                                  iota_c[:, :].rearrange("p (a c) -> p a c", a=1).to_broadcast([P, 4, P]),
                                  pos_f[:, 4 * m:4 * m + 4].rearrange("p (s a) -> p s a", a=1).to_broadcast([P, 4, P]),
                                  ALU.is_equal).then_inc(s_pos, 1)
            c8 = cmp8.rearrange("p (c e) -> p c e", e=E)
            cols = iota_c[:, 0:NCOL].rearrange("p (c a) -> p c a", a=1)
            step(dve.tensor_tensor(c8, tend.rearrange("p (a e) -> p a e", a=1).to_broadcast([P, NCOL, E]),
                                   cols.to_broadcast([P, NCOL, E]), ALU.is_le))
            step(dve.tensor_reduce(eid_f, c8, AX.X, ALU.add))
            step(dve.tensor_scalar(eid_f, eid_f, float(E - 1), None, ALU.min))
            step(dve.tensor_copy(eid[:, :], eid_f))
            step(dve.tensor_tensor(c8[:, :, 0:E - 2], tstart[:, 1:E - 1].rearrange("p (a e) -> p a e", a=1)
                                   .to_broadcast([P, NCOL, E - 2]), cols.to_broadcast([P, NCOL, E - 2]), ALU.is_equal))
            step(dve.tensor_reduce(eid_f, c8[:, :, 0:E - 2], AX.X, ALU.add))
            step(dve.tensor_copy(first[:, :], eid_f))
            dve.wait_ge(s_posu, 2 * NT // 4)
            step(dve.tensor_copy(dtab, table_ps))
            step(dve.scalar_tensor_tensor(dpad, dtab, 0.0, pad_row, ALU.is_equal, ALU.mult))
            step(dve.tensor_scalar(dtab, dtab, -1.0, None, ALU.add))
            step(dve.tensor_scalar(dtok, dtab, float(NTOK), float(-NTOK), ALU.is_ge, ALU.mult))
            step(dve.tensor_tensor(dtok, dtok, dtab, ALU.add))
            step(dve.tensor_scalar(gidx[:, :], dtok, 0.0, None, ALU.max))
            step(dve.tensor_tensor(dpad, dpad, dtab, ALU.add))
            dve.tensor_copy(sidx[:, :], dpad).then_inc(s_idx, 1)
            dve.wait_ge(s_idx, 1)
            dve.wait_ge(s_u0b, 2)
            step(dve.tensor_tensor(u0t[:, 5, :], u0t[:, 3, :], u0t[:, 4, :], ALU.subtract))
            for b in range(B):
                step(dve.tensor_tensor(u0[:, :].rearrange("p (q b) -> p q b", b=B)[:, :, b], u0t[:, 5, :],
                                       u0t[:, 0, :], ALU.add))

            with dve.Fori(0, NCH) as c:
                dve.wait_ge(s_k, c + 1)
                dve.wait_ge(s_U, c + 1)
                dve.wait_ge(s_e, 5 * c + 2)
                for q in range(Q):
                    dve.tensor_scalar(nn[:, q * CH:(q + 1) * CH], yh_ps[:, q * CH:(q + 1) * CH],
                                      bias_sb[:, 1, q:q + 1], 0.0, ALU.add, ALU.min).then_inc(s_n, 1)
                dve.wait_ge(s_l1, c + 1)
                dve.scalar_tensor_tensor(l1, kb, 0.0, l1, ALU.max, ALU.add).then_inc(s_c, 1)
                dve.wait_ge(s_u1, c + 1)
                dve.tensor_tensor(l3, l3, nn, ALU.add).then_inc(s_ua, 1)
                dve.wait_ge(s_u2, c + 1)
                dve.wait_ge(s_acp, c + 2)
                dve.tensor_tensor(kb, kb, cum_ps, ALU.add).then_inc(s_ua, 1)
                dve.wait_ge(s_ua, 2 * c + 2)
                dve.tensor_tensor(U[:, :].rearrange("p (q n) -> p q n", q=Q)[:, :, ds(c * CH, CH)],
                                  l3.rearrange("p (q n) -> p q n", q=Q), kb.rearrange("p (q n) -> p q n", q=Q),
                                  ALU.add).then_inc(s_U, 1)

            def x_lo(j, slot):
                dve.wait_ge(s_xhi, j + 1)
                dve.tensor_tensor(xT[:, slot, 1, :], xT_ps, xT[:, slot, 0, :].bitcast(fp32),
                                  ALU.subtract).then_inc(s_xlo, 1)

            def h_lo(j):
                dve.wait_ge(s_hhi, j + 1)
                dve.tensor_tensor(hT[:, 1, :], hT_ps, hT[:, 0, :].bitcast(fp32), ALU.subtract).then_inc(s_hlo, 1)

            def gate(j):
                dve.wait_ge(s_silu, j + 1)
                dve.tensor_tensor(g_h, sl, up_ps[:, F:2 * F], ALU.mult).then_inc(s_g, 1)

            x_lo(0, 0)
            gate(0)
            x_lo(1, 1)
            h_lo(0)
            dve.wait_ge(s_k, NCH)
            step(dve.tensor_copy(M[:, :, 0], u0[:, :]))
            dve.wait_ge(s_raw, 64)
            dve.tensor_copy(wbuf[:, 1, 0, :], raw[:, :]).then_inc(s_hi, 1)

            def tile_step(j, u, hook=None):
                dve.wait_ge(s_ht, j)
                gate(j)
                x_lo(j + 1, 0 if u == 0 else 1)
                h_lo(j)
                if hook:
                    hook()
                starts = dve.value_load(first[0:1, ds(j, 1)], min_val=0, max_val=1)
                e = dve.value_load(eid[0:1, ds(j, 1)], min_val=0, max_val=E - 1)
                with dve.If(starts > 0):
                    dve.wait_ge(s_raw, 32 * e + 64)
                    dve.wait_ge(s_dn, j)
                    dve.tensor_copy(wslot(e + 1, 0, 0, WALL), raw[:, :]).then_inc(s_hi, 1)

            def run_max(i):
                def run():
                    row = Ug[:, ds(i, 1), :].rearrange("p a t -> p (a t)")
                    dve.tensor_tensor_scan(M[:, ds(i, 1), 1:T + 1].rearrange("p a t -> p (a t)"), row, row,
                                           u0[:, ds(i, 1)], ALU.max, ALU.max).then_inc(s_M, 1)
                    dve.wait_ge(s_M, i + 1)
                    dve.tensor_tensor(Dm.rearrange("p (a t) -> p a t", a=1), M[:, ds(i, 1), 0:T],
                                      M[:, ds(i, 1), 1:T + 1], ALU.subtract).then_inc(s_D, 1)
                return run

            def run_scan(i):
                def run():
                    dve.wait_ge(s_De, i + 1)
                    dve.wait_ge(s_Ee, i + 1)
                    dve.tensor_tensor_scan(Sm, Dm, Ug[:, ds(i, 1), :].rearrange("p a t -> p (a t)"), 1.0,
                                           ALU.mult, ALU.add).then_inc(s_S, 1)
                return run

            def sums():
                dve.wait_ge(s_lh, 4)
                for m in range(8):
                    ins = dve.bn_stats(gst[:, m, :], A[:, 512 * m:512 * (m + 1)])
                step(ins)
                step(dve.bn_aggr(gs[:, 0:2], gst[:, :, :].rearrange("p a b -> p (a b)")))
                step(dve.tensor_reduce(gs[:, 2:3], u0[:, :], AX.X, ALU.add))
                dve.scalar_tensor_tensor(gs[:, 3:4], gs[:, 0:1], float(2 * NTOK), gs[:, 2:3], ALU.mult,
                                         ALU.add).then_inc(s_mean_in, 1)

            def squares():
                dve.wait_ge(s_mean, 1)
                step(dve.tensor_scalar(gs[:, 4:5], stat_ps[:, 0:1], 1.0 / NSTAT, None, ALU.mult))
                step(dve.tensor_scalar(gs[:, 5:6], gs[:, 0:1], gs[:, 4:5], None, ALU.subtract))
                step(dve.scalar_tensor_tensor(gs[:, 6:7], gs[:, 5:6], gs[:, 5:6], gs[:, 1:2], ALU.mult, ALU.add))
                step(dve.tensor_scalar(gs[:, 10:14], u0[:, :], gs[:, 4:5], None, ALU.subtract))
                step(dve.tensor_tensor(gs[:, 10:14], gs[:, 10:14], gs[:, 10:14], ALU.mult))
                step(dve.tensor_reduce(gs[:, 14:15], gs[:, 10:14], AX.X, ALU.add))
                dve.scalar_tensor_tensor(gs[:, 7:8], gs[:, 6:7], float(2 * NTOK), gs[:, 14:15], ALU.mult,
                                         ALU.add).then_inc(s_var_in, 1)

            def normaliser():
                dve.wait_ge(s_std, 1)
                step(dve.reciprocal(gs[:, 8:9], gs[:, 15:16]))
                step(dve.scalar_tensor_tensor(gs[:, 9:10], gs[:, 4:5], -1.0, gs[:, 8:9], ALU.mult, ALU.mult))
                dve.sem_inc(s_norm, 1)

            def row_stats(m):
                def run():
                    rows = xn[:, ds(2 * m, 2), :]
                    dve.wait_ge(s_htr, m + 2)
                    dve.tensor_tensor(rtmp[:, :, :], tr_ps.rearrange("p (t d) -> p t d", t=2), rows, ALU.add).then_inc(s_p1, 1)
                    hold(dve, s_p1, 4 * m + 2)
                    dve.tensor_copy(rows, rtmp[:, :, :])
                    for t in range(2):
                        ins = dve.bn_stats(st3[:, t, :], rtmp[:, t, :])
                    ins.then_inc(s_p1, 1)
                    hold(dve, s_p1, 4 * m + 3)
                    for t in range(2):
                        ins = dve.bn_aggr(mv3[:, t, :], st3[:, t, :])
                    ins.then_inc(s_p1, 1)
                    dve.wait_ge(s_p1, 4 * m + 4)
                    dve.tensor_copy(mv[:, ds(2 * m, 2), :], mv3[:, :, :]).then_inc(s_p1, 1)
                return run

            def last_norm(m):
                def run():
                    rows = xn[:, ds(2 * m, 2), :]
                    for t in range(2):
                        row = xn[:, ds(2 * m + t, 1), :].rearrange("p a d -> p (a d)")
                        ins = dve.tensor_scalar(row, row, mv[:, ds(2 * m + t, 1), 0:1].rearrange("p a b -> p (a b)"),
                                                rstd[:, ds(2 * m + t, 1)], ALU.subtract, ALU.mult)
                    ins.then_inc(s_p2, 1)
                    dve.wait_ge(s_p2, 4 * m + 2)
                    for k in range(2):
                        dve.tensor_tensor(rows, rows, lnwb[:, k:k + 1, :].to_broadcast([P, 2, D]),
                                          ALU.add if k else ALU.mult).then_inc(s_p2, 1)
                        dve.wait_ge(s_p2, 4 * m + (3 + k))
                    dve.wait_ge(s_xre, 16 * m + 16)
                    dve.tensor_tensor(rows, rows, xre[:, :, :], ALU.add).then_inc(s_p2, 1)
                return run

            with dve.Fori(0, 4) as i:
                tile_step(2 * i + 1, 0, run_max(i))
                tile_step(2 * i + 2, 1, run_scan(i))
            tile_step(9, 0, sums)
            tile_step(10, 1)
            squares()
            tile_step(11, 0)
            normaliser()
            tile_step(12, 1)
            with dve.Fori(6, 10) as i:
                tile_step(2 * i + 1, 0, row_stats(2 * i - 12))
                tile_step(2 * i + 2, 1, row_stats(2 * i - 11))
            dve.wait_ge(s_std3, 1)
            step(dve.reciprocal(rstd[:, :], std[:, :]))
            with dve.Fori(10, 14) as i:
                tile_step(2 * i + 1, 0, last_norm(2 * i - 20))
                tile_step(2 * i + 2, 1, last_norm(2 * i - 19))
            with dve.Fori(14, (NTILES - 1) // 2) as i:
                tile_step(2 * i + 1, 0)
                tile_step(2 * i + 2, 1)
            for g in range(4):
                dve.wait_ge(s_yl[g], 32)
                for t in range(4 * g, 4 * g + 4):
                    ins = dve.scalar_tensor_tensor(xn[:, t, :], U[:, D * t:D * (t + 1)], w12[:, 0, t:t + 1],
                                                   xn[:, t, :], ALU.mult, ALU.add)
                step(ins)
                for t in range(4 * g, 4 * g + 4):
                    ins = dve.scalar_tensor_tensor(xn[:, t, :], A[:, D * t:D * (t + 1)], w12[:, 1, t:t + 1],
                                                   xn[:, t, :], ALU.mult, ALU.add)
                ins.then_inc(s_fin, 1)

        @block.tensor
        def _(pe):
            pe.wait_ge(s_const, 14)
            pe.wait_ge(s_small, 32)
            for m in range(NT // 2):
                pe.wait_ge(s_xn, m // 2 + 1)
                if m >= 2:
                    pe.wait_ge(s_xnT, m - 1)
                for t in range(2):
                    for q in range(Q):
                        col = (4 + m % 2) * 512 + (t * Q + q) * P
                        ins = pe.transpose(PS[:, col:col + P], xn[:, 2 * m + t, q * P:(q + 1) * P], ident[:, :])
                ins.then_inc(s_xtr, 1)
            for t in range(NT):
                pe.wait_ge(s_xnT, t // 2 + 1)
                for q in range(Q):
                    ins = pe.matmul(logit_ps[:, t * E:(t + 1) * E], xnT[:, q, t * P:(t + 1) * P], wg_sb[:, q, :],
                                    start=(q == 0), stop=(q == Q - 1))
            ins.then_inc(s_lg, 1)

            def project(c):
                for mat, base in ((0, 0), (1, 2 * CH)):
                    for qo in range(Q):
                        for q in range(Q):
                            ins = pe.matmul(PS[:, base + qo * CH:base + (qo + 1) * CH],
                                            wzh_sb[:, q, mat, qo * P:(qo + 1) * P], xnT[:, q, ds(c * CH, CH)],
                                            start=(q == 0), stop=(q == Q - 1))
                ins.then_inc(s_k, 1)

            def cumsum(c):
                pe.wait_ge(s_c, c + 1)
                pe.wait_ge(s_acp, c + 1)
                pe.wait_ge(s_U, c + 1)
                pe.matmul(cum_ps[:, 0:CH], tri[:, :], l1[:, 0:CH], start=True, stop=True)
                pe.matmul(cum_ps[:, CH:2 * CH], ones[:, :], l1[:, 0:CH], start=True, stop=False)
                pe.matmul(cum_ps[:, CH:2 * CH], tri[:, :], l1[:, CH:2 * CH], start=False,
                          stop=True).then_inc(s_cum, 1)
            project(0)
            pe.wait_ge(s_pick, 1)
            pe.matmul(rank_ps, tri_b[:, :], pick_b[:, :], start=True, stop=True)
            pe.matmul(tot_ps, ones_b[:, :], pick_b[:, :], start=True, stop=True).then_inc(s_rank, 1)
            for m in range(2 * NT // 4):
                pe.wait_ge(s_pos, m + 1)
                for s in range(4):
                    r = 4 * m + s
                    ins = pe.matmul(table_ps, onehot_pos[:, m % 2, s * P:(s + 1) * P],
                                    onehot_tile[:, r * NCOL:(r + 1) * NCOL], start=(r == 0), stop=(r == 2 * NT - 1))
                ins.then_inc(s_posu, 1)
            cumsum(0)
            with pe.Fori(1, NCH) as c:
                pe.wait_ge(s_n, 2 * c)
                pe.wait_ge(s_l1, c)
                project(c)
                cumsum(c)

            def x_tile(j, slot, s, val):
                pe.wait_ge(s, val)
                for q in range(Q):
                    ins = pe.transpose(xT_ps[:, q * P:(q + 1) * P], xg[:, slot, q * P:(q + 1) * P], ident[:, :])
                ins.then_inc(s_xt, 1)

            def up(j, slot, e):
                pe.wait_ge(s_xlo, j + 1)
                pe.wait_ge(s_w, e + 1)
                for q in range(Q):
                    for xpart, wpart in ((0, 0), (0, 1), (1, 0)):
                        for a, b in UP_PIECES:
                            ins = pe.matmul(up_ps[:, a:b], xT[:, slot, xpart, q * P:(q + 1) * P],
                                            wslot(e, wpart, q * 2 * F + a, q * 2 * F + b),
                                            start=(q == 0 and xpart == 0 and wpart == 0),
                                            stop=(q == Q - 1 and xpart == 1))
                ins.then_inc(s_up, 1)

            def down(j, e):
                pe.wait_ge(s_hlo, j + 1)
                pe.wait_ge(s_y, j + 1)
                for c in range(HC):
                    for hpart, wpart in ((0, 0), (0, 1), (1, 0)):
                        ins = pe.matmul(y_ps, hT[:, hpart, c * P:(c + 1) * P],
                                        wslot(e, wpart, W13 + c * D, W13 + (c + 1) * D),
                                        start=(c == 0 and hpart == 0 and wpart == 0),
                                        stop=(c == HC - 1 and hpart == 1))
                ins.then_inc(s_dn, 1)

            def h_tile(j):
                pe.wait_ge(s_g, j + 1)
                for c in range(HC):
                    a = min(c * P, F - P)
                    ins = pe.transpose(hT_ps[:, c * P:(c + 1) * P], g_h[:, a:a + P], ident[:, :])
                ins.then_inc(s_ht, 1)

            pe.wait_ge(s_acp, NCH + 1)
            pe.wait_ge(s_U, NCH + 1)
            x_tile(0, 0, s_ga, 16)
            up(0, 0, 0)
            x_tile(1, 1, s_gb, 16)
            h_tile(0)

            def pair(i, hooks=(None, None)):
                e = [pe.value_load(eid[0:1, ds(2 * i + k, 1)], min_val=0, max_val=E - 1) for k in range(3)]
                for u in range(2):
                    j = 2 * i + (1 + u)
                    pe.wait_ge(s_g, j)
                    up(j, 1 - u, e[u + 1])
                    x_tile(j + 1, u, s_ga if u == 0 else s_gb, 16 * i + 32)
                    down(j - 1, e[u])
                    h_tile(j)
                    if hooks[u]:
                        hooks[u]()

            def sum_all(src, col, s_in, s_out):
                def run():
                    pe.wait_ge(s_in, 1)
                    pe.matmul(stat_ps[:, col:col + 1], ones[:, :], src, start=True, stop=True).then_inc(s_out, 1)
                return run

            def h_back(m):
                def run():
                    pe.wait_ge(s_h, m + 1)
                    pe.wait_ge(s_p1, 4 * m + 1)
                    for t in range(2):
                        for q in range(Q):
                            col = (t * Q + q) * P
                            ins = pe.transpose(tr_ps[:, col:col + P], hst[:, q, t * P:(t + 1) * P], ident[:, :])
                    ins.then_inc(s_htr, 1)
                return run
            with pe.Fori(0, 4) as i:
                pair(i)
            pair(4, (None, sum_all(gs[:, 3:4], 0, s_mean_in, s_mean)))
            pair(5, (sum_all(gs[:, 7:8], 2, s_var_in, s_var), None))
            with pe.Fori(6, 10) as i:
                pair(i, (h_back(2 * i - 12), h_back(2 * i - 11)))
            with pe.Fori(10, (NTILES - 1) // 2) as i:
                pair(i)
            e = pe.value_load(eid[0:1, NTILES - 1:NTILES], min_val=0, max_val=E - 1)
            down(NTILES - 1, e)




def kernel(**inputs):
    import numpy as _np
    import concourse.bacc as _bacc
    from concourse import mybir as _mybir
    from concourse.bass_utils import run_bass_kernel_spmd as _run

    a = {k: _np.ascontiguousarray(v) for k, v in inputs.items()}
    w1, w2, w3 = a["L0_ffn_w1"], a["L0_ffn_w2"], a["L0_ffn_w3"]
    up = _np.concatenate([w1, w3], 1).transpose(0, 2, 1).reshape(E, Q, P, 2 * F).transpose(0, 2, 1, 3)
    dn = w2.transpose(0, 2, 1)
    main = _np.concatenate([up.reshape(E, P, W13),
                            dn[:, 0:FULL * P].reshape(E, FULL, P, D).transpose(0, 2, 1, 3).reshape(E, P, FULL * D)], 2)
    zh = _np.stack([a["L0_attn_W_z"].T, a["L0_attn_W_h"].T], 1)
    arrays = {
        "x": a["L0_attn_hidden_states"].reshape(NTOK, D),
        "wzh": zh.reshape(Q, P, 2, D).transpose(1, 0, 2, 3),
        "bias": _np.stack([a["L0_attn_b_z"], a["L0_attn_b_h"]]).reshape(2, Q, P).transpose(2, 0, 1),
        "h0": a["L0_attn_h0"].reshape(Q, P).T,
        "ln_wb": _np.stack([a["L0_attn_ln_w"], a["L0_attn_ln_b"]])[None].repeat(P, 0),
        "wg": a["L0_ffn_w_gate"].T.reshape(Q, P, E).transpose(1, 0, 2),
        "w_main": main,
        "w_tail": dn[:, FULL * P:],
    }
    arrays = {k: _np.ascontiguousarray(v) for k, v in arrays.items()}
    nc = _bacc.Bacc("TRN2", target_bir_lowering=False, num_devices=1)
    f32 = _mybir.dt.float32
    args = [nc.dram_tensor(n, v.shape, f32, kind="ExternalInput").ap() for n, v in arrays.items()]
    args.append(nc.dram_tensor("out", [NTOK, D], f32, kind="ExternalOutput").ap())
    args.append(nc.dram_tensor("xn_dram", [NTOK, D], f32).ap())
    args.append(nc.dram_tensor("y_dram", [2 * NTOK + 4 * P, D], f32).ap())
    build_program(nc, *args)
    r = _run(nc, [arrays], core_ids=[0])
    return r.results[0]["out"].reshape(B, T, D)
```

```python
import concourse.bass as bass
from concourse import mybir
from contextlib import ExitStack

P = 128
B, T, D = 2, 1024, 256
NTOK = B * T
NT = NTOK // P
Q = D // P
E, F = 8, 704
NTILES = (2 * NTOK + E * (P - 1)) // P
AT = (0, 0, 1, 2)
DEEP = 4
NCOL = -(-NTILES // DEEP) * DEEP + DEEP
LOOP = 4
FULL = F // P
HC = FULL + 1
TAIL = F - FULL * P
W13 = Q * 2 * F
WMAIN = W13 + FULL * D
WALL = WMAIN + D
LOADS = 5 * 16
PIECES = 4
WP = WALL // PIECES
SMALL = [("wzh", Q * 2 * D), ("wg", Q * E), ("bias", 2 * Q), ("h0", Q), ("ln", 2 * D)]
CH = 512
NCH = NTOK // CH
LN_EPS = 1e-5
NSTAT = B * (T + 1) * D
SCRATCH = 2 * NTOK
UP_PIECES = [(0, 512), (512, 1024), (1024, 1408)]
BIG = 3.0e38


def build_program(nc, x, small, w_main, w_tail, out, xn_dram, y_dram):
    fp32, f32r, i32 = mybir.dt.float32, mybir.dt.float32r, mybir.dt.int32
    u32, bf16 = mybir.dt.uint32, mybir.dt.bfloat16
    ALU, ACT, AX = mybir.AluOpType, mybir.ActivationFunctionType, mybir.AxisListType
    ds = bass.ds
    ctx = ExitStack()
    with ctx:
        def sb(name, shape, dt=fp32):
            return ctx.enter_context(nc.sbuf_tensor(name, shape, dt))

        def sem(name):
            return ctx.enter_context(nc.semaphore(name))

        xn = sb("xn", [P, NT, D])
        xnT_M = sb("xnT_M", [P, 4 * (T + 1)])
        xnT = xnT_M[:, 0:Q * NTOK].rearrange("p (q n) -> p q n", q=Q)
        M = xnT_M[:, :].rearrange("p (g t) -> p g t", g=4)
        U = sb("U", [P, 2 * NTOK])
        Ug = U[:, :].rearrange("p (g t) -> p g t", g=4)
        A = sb("A", [P, 2 * NTOK])
        Ag = A[:, :].rearrange("p (g t) -> p g t", g=4)
        wbuf = sb("wbuf", [P, 2, 2, WALL], f32r)
        wflat = wbuf[:, :, :, :].rearrange("p s h n -> p (s h n)")
        raw = sb("raw", [P, WALL])
        tmp = sb("tmp", [P, 6, Q * CH])
        tflat = tmp[:, :, :].rearrange("p a n -> p (a n)")
        l2 = tmp[:, 4, :]
        sets = [[tmp[:, n, :] for n in range(4)], [raw[:, n * Q * CH:(n + 1) * Q * CH] for n in range(4)]]
        g_h = tflat[:, 0:F]
        sl = tflat[:, F:2 * F]
        Dg = tmp[:, 2:6, :]
        rtmp, xre = (tmp[:, 5, k * 2 * D:(k + 1) * 2 * D].rearrange("p (t d) -> p t d", t=2) for k in range(2))
        hst = sb("hst", [P, Q, 2 * P])
        eps = sb("eps", [P, 1])
        hT = sb("hT", [P, 2, HC * P], f32r)
        xT = sb("xT", [P, 2, 2, D], f32r)
        onehot_tile = hT[:, :, :].rearrange("p a n -> p (a n)")[:, 0:2 * NT * NCOL]
        onehot_pos = xT[:, :, :, :].rearrange("p a b n -> p a (b n)")
        xg = sb("xg", [P, DEEP, D])
        ysb = sb("ysb", [P, DEEP, D])
        small_sb = sb("small_sb", [P, sum(n for _, n in SMALL)])
        where, start = {}, 0
        for name, n in SMALL:
            where[name] = small_sb[:, start:start + n]
            start += n
        wzh_sb = where["wzh"].rearrange("p (q m d) -> p q m d", q=Q, m=2)
        wg_sb = where["wg"].rearrange("p (q e) -> p q e", q=Q)
        bias_sb = where["bias"].rearrange("p (m q) -> p m q", m=2)
        h0_sb = where["h0"]
        lnwb = where["ln"].rearrange("p (m d) -> p m d", m=2)
        nbias = sb("nbias", [P, Q])
        nmean = sb("nmean", [P, NT])
        ident = sb("ident", [P, P])
        tri = sb("tri", [P, P])
        ones = sb("ones", [P, P])
        tri_b = sb("tri_b", [P, P], bf16)
        ones_b = sb("ones_b", [P, P], bf16)
        pick_b = sb("pick_b", [P, NT * E], bf16)
        iota_c = sb("iota_c", [P, P])
        bst = sb("bst", [P, NT, 6])
        mv = sb("mv", [P, NT, 2])
        rstd = sb("rstd", [P, NT])
        w12 = sb("w12", [P, 2, NT])
        slot_i = sb("slot_i", [P, 3, 2 * NT], i32)
        gcol = sb("gcol", [P, DEEP], u32)
        scol = sb("scol", [P, DEEP], u32)
        gidx = sb("gidx", [P, NCOL], u32)
        sidx = sb("sidx", [P, NCOL], u32)
        eid = sb("eid", [P, NCOL], i32)
        plan = sb("plan", [P, NCOL + 1], i32)
        u0 = sb("u0", [P, 4])
        u0t = sb("u0t", [P, 6, Q])
        gst = sb("gst", [P, 8, 6])
        gs = sb("gs", [P, 16])
        st3 = sb("st3", [P, 2, 6])
        mv3 = sb("mv3", [P, 2, 2])
        std = sb("std", [P, NT])
        at = [0]

        def ut(cols):
            at[0] += cols
            return U[:, at[0] - cols:at[0]]
        logit = ut(NT * E)
        t_a, t_b, hot1, hot2, pick, slots = (ut(NT * E) for _ in range(6))
        tot = ut(E * NT)
        cum = ut(E * NT)
        keep = ut(E * NT)
        m12 = ut(2 * NT)
        idx8 = ut(NT)
        slot_f, pos_f, tile_f, id_f = (ut(2 * NT) for _ in range(4))
        cnt, one8 = (ut(E) for _ in range(2))
        thr = ut(E * NT)
        dtab, dpad, dtok = (ut(NCOL) for _ in range(3))
        pad_row = ut(NCOL)
        hflat = hst[:, :, :].rearrange("p q n -> p (q n)")
        ht_at = [0]

        def pt(cols):
            ht_at[0] += cols
            return hflat[:, ht_at[0] - cols:ht_at[0]]
        cmp8 = pt(NCOL * E)
        ntile, tend, tstart, last = (pt(E) for _ in range(4))
        when = pt(3 * (E - 1))
        due = U[:, 2 * CH:2 * CH + NCOL * 3 * (E - 1)]
        plan_f, eid_f = pt(NCOL + 1), pt(NCOL)

        PS = ctx.enter_context(nc.psum_tensor("PS", [P, 8 * 512], fp32))
        up_ps = PS[:, 0:2 * F]
        hT_ps = PS[:, 3 * 512:3 * 512 + HC * P]
        xT_ps = PS[:, 5 * 512:5 * 512 + D]
        y_ps = PS[:, 6 * 512:6 * 512 + D]
        tr_ps = PS[:, 7 * 512:8 * 512]
        k_ps = PS[:, 0:2 * CH]
        yh_ps = PS[:, 2 * CH:4 * CH]
        cum_ps = PS[:, 4 * CH:6 * CH]
        rank_ps = PS[:, 6 * 512:6 * 512 + NT * E]
        tot_ps = PS[:, 6 * 512 + 128:6 * 512 + 128 + NT * E]
        table_ps = PS[:, 6 * 512 + 256:6 * 512 + 256 + NCOL]
        stat_ps = PS[:, 7 * 512:7 * 512 + 4]
        logit_ps = PS[:, 7 * 512:7 * 512 + NT * E]

        s_x = [sem(f"x_loaded{g}") for g in range(4)]
        s_small = sem("small_inputs_loaded")
        s_raw = sem("expert_loaded")
        s_const = sem("constants_made")
        s_pool = sem("pool_steps")
        s_dve = sem("dve_steps")
        s_act = sem("act_steps")
        s_xn = sem("xn_group_ready")
        s_xnd = sem("xn_stored")
        s_xtr = sem("xn_transposed")
        s_xnT = sem("xnT_ready")
        s_lg = sem("logits_done")
        s_mr = sem("group_scales_ready")
        s_pick = sem("picks_ready")
        s_rank = sem("ranks_done")
        s_pos = sem("onehots_ready")
        s_posu = sem("onehots_used")
        s_idx = sem("tables_ready")
        s_ctl = sem("tile_plan_ready")
        s_zin = sem("gap_ready")
        s_zex = sem("gap_exp_done")
        s_u0a = sem("u0_exp_done")
        s_u0b = sem("u0_logs_done")
        s_u0i = sem("u0_inputs_ready")
        s_nb = sem("minus_b_h_ready")
        s_kp = sem("k_projected")
        s_k = sem("k_and_h_projected")
        s_kb = sem("kb_ready")
        s_yr = sem("k_and_h_read")
        s_e = sem("act_chain")
        s_l1 = sem("l1_ready")
        s_l3 = sem("l3_ready")
        s_l2 = sem("l2_ready")
        s_c = sem("c_ready")
        s_cum = sem("cumsum_done")
        s_acp = sem("a_star_copied")
        s_u1 = sem("l3_minus_l2_ready")
        s_u2 = sem("k_minus_c_ready")
        s_u3 = sem("k_minus_c_plus_cumsum_ready")
        s_ua = sem("h_part_ready")
        s_U = sem("u_ready")
        s_hi = sem("hi_pieces_ready")
        s_w = sem("expert_pieces_ready")
        s_gt = [sem(f"gathered{k}") for k in range(DEEP)]
        s_gc = sem("gather_column_ready")
        s_sc = sem("scatter_column_ready")
        s_xt = sem("x_tile_transposed")
        s_xhi = sem("x_hi_ready")
        s_xlo = sem("x_lo_ready")
        s_up = sem("up_done")
        s_silu = sem("silu_ready")
        s_g = sem("gated_ready")
        s_ht = sem("gated_transposed")
        s_hhi = sem("h_hi_ready")
        s_hlo = sem("h_lo_ready")
        s_dn = sem("down_done")
        s_y = sem("y_copied")
        s_st = [sem(f"scattered{k}") for k in range(DEEP)]
        s_M = sem("running_max_ready")
        s_D = sem("max_steps_ready")
        s_Em = sem("u_minus_max_ready")
        s_De = sem("decay_ready")
        s_Ee = sem("increment_ready")
        s_S = sem("scan_ready")
        s_lS = sem("log_scan_ready")
        s_L = sem("log_plus_max_ready")
        s_lh = sem("log_h_ready")
        s_mean_in = sem("sums_ready")
        s_mean = sem("mean_summed")
        s_var_in = sem("squares_ready")
        s_var = sem("squares_summed")
        s_norm = sem("norm_ready")
        s_xre = sem("x_loaded_again")
        s_hx = sem("h_exp_done")
        s_h = sem("h_ready")
        s_htr = sem("h_transposed")
        s_p1 = sem("stats_steps")
        s_p2 = sem("last_norm_steps")
        s_var0 = sem("group_variance_ready")
        s_std0 = sem("group_deviation_ready")
        s_std = sem("log_h_deviation_ready")
        s_std3 = sem("row_deviations_ready")
        s_yl = [sem(f"y_loaded{g}") for g in range(4)]
        s_fin = sem("result_ready")
        s_out = sem("result_stored")

        block = ctx.enter_context(nc.Block())

        def hold(eng, s, value):
            eng.wait_ge(s, value)
            eng.nop(nofuse=True)

        def wslot(e, part, a):
            return wflat[:, ds(e % 2 * (2 * WALL) + (a + part * WALL), WP)]

        @block.sync
        def _(sp):
            for g in range(4):
                sp.dma_start(xn[:, 4 * g:4 * g + 4, :],
                             x[512 * g:512 * (g + 1), :].rearrange("(t p) d -> p t d", p=P)).then_inc(s_x[g], 16)
            for q in range(PIECES - 1):
                sp.dma_start(raw[:, q * WP:(q + 1) * WP], w_main[0][:, q * WP:(q + 1) * WP]).then_inc(s_raw, 16)
            sp.dma_start(raw[:, WP * (PIECES - 1):WMAIN], w_main[0][:, WP * (PIECES - 1):WMAIN]).then_inc(s_raw, 16)
            sp.dma_start(raw[P - TAIL:P, WMAIN:WALL], w_tail[0]).then_inc(s_raw, 16)
            for g in range(4):
                sp.wait_ge(s_xn, g + 1)
                sp.dma_start(xn_dram[512 * g:512 * (g + 1), :].rearrange("(t p) d -> p t d", p=P),
                             xn[:, 4 * g:4 * g + 4, :]).then_inc(s_xnd, 16)
            sp.wait_ge(s_U, NCH)
            with sp.Fori(1, E) as e:
                def row(w, a, b):
                    return w[ds(e, 1)][:, :, a:b].rearrange("a p n -> (a p) n")
                for q in range(PIECES):
                    sp.wait_ge(s_w, PIECES * e - (PIECES - 1) + q)
                    sp.dma_start(raw[:, q * WP:min((q + 1) * WP, WMAIN)],
                                 row(w_main, q * WP, min((q + 1) * WP, WMAIN))).then_inc(s_raw, 16)
                sp.dma_start(raw[P - TAIL:P, WMAIN:WALL], row(w_tail, 0, D)).then_inc(s_raw, 16)
            for k in range(DEEP):
                sp.wait_ge(s_st[k], 16 * (len(range(k, NTILES, DEEP)) + 1))
            for g in range(4):
                for k, buf in ((0, U), (1, A)):
                    sp.dma_start(buf[:, 1024 * g:1024 * (g + 1)].rearrange("p (t d) -> p t d", d=D),
                                 y_dram[k * NTOK + 512 * g:k * NTOK + 512 * (g + 1), :]
                                 .rearrange("(t p) d -> p t d", p=P)).then_inc(s_yl[g], 16)
            for g in range(4):
                sp.wait_ge(s_fin, g + 1)
                sp.dma_start(out[512 * g:512 * (g + 1), :].rearrange("(t p) d -> p t d", p=P),
                             xn[:, 4 * g:4 * g + 4, :]).then_inc(s_out, 16)
            sp.wait_ge(s_out, 64)

        @block.gpsimd
        def _(pool):
            n = [0]

            def step(ins):
                n[0] += 1
                ins.then_inc(s_pool, 1)
                pool.wait_ge(s_pool, n[0])
            pool.memset(ident[:, :], 0.0).then_inc(s_const, 1)
            pool.memset(ones[:, :], 1.0).then_inc(s_const, 1)
            pool.memset(tri[:, :], 1.0).then_inc(s_const, 1)
            pool.memset(ones_b[:, :], 1.0).then_inc(s_const, 1)
            pool.memset(tri_b[:, :], 1.0).then_inc(s_const, 1)
            pool.memset(raw[0:P - TAIL, WMAIN:WALL], 0.0).then_inc(s_const, 1)
            pool.wait_ge(s_const, 6)
            pool.affine_select(out=ident[:, :], in_=ident[:, :], compare_op=ALU.not_equal, fill=1.0, base=0,
                               pattern=[[-1, P]], channel_multiplier=1).then_inc(s_const, 1)
            pool.affine_select(out=tri[:, :], in_=tri[:, :], compare_op=ALU.is_ge, fill=0.0, base=0,
                               pattern=[[1, P]], channel_multiplier=-1).then_inc(s_const, 1)
            pool.affine_select(out=tri_b[:, :], in_=tri_b[:, :], compare_op=ALU.is_gt, fill=0.0, base=0,
                               pattern=[[1, P]], channel_multiplier=-1).then_inc(s_const, 1)
            pool.iota(iota_c[:, :], [[1, P]], base=0, channel_multiplier=0,
                      allow_small_or_imprecise_dtypes=True).then_inc(s_const, 1)
            pool.iota(id_f.rearrange("p (k t) -> p k t", k=2), [[NTOK, 2], [P, NT]], base=1, channel_multiplier=1,
                      allow_small_or_imprecise_dtypes=True).then_inc(s_const, 1)
            pool.iota(pad_row.rearrange("p (c u) -> p c u", u=DEEP), [[0, NCOL // DEEP], [P, DEEP]], base=SCRATCH + 1,
                      channel_multiplier=1, allow_small_or_imprecise_dtypes=True).then_inc(s_const, 1)
            pool.memset(eps[:, :], LN_EPS).then_inc(s_const, 1)
            pool.memset(ysb[:, :, :], 0.0).then_inc(s_const, 1)
            pool.wait_ge(s_const, 14)
            for k in range(DEEP):
                pool.dma_start(y_dram[SCRATCH + (DEEP + k) * P:SCRATCH + (DEEP + k + 1) * P, :],
                               ysb[:, k, :]).then_inc(s_st[k], 16)
            for g in range(4):
                pool.wait_ge(s_mr, g + 1)
                for t in range(4 * g, 4 * g + 4):
                    ins = pool.tensor_scalar(xn[:, t, :], xn[:, t, :], rstd[:, t:t + 1], nmean[:, t:t + 1],
                                             ALU.mult, ALU.add)
                ins.then_inc(s_xn, 1)

            for q in range(PIECES):
                pool.wait_ge(s_hi, q + 1)
                lo, hi = (wbuf[:, 0, n, q * WP:(q + 1) * WP] for n in (1, 0))
                pool.tensor_tensor(lo, raw[:, q * WP:(q + 1) * WP], hi.bitcast(fp32), ALU.subtract).then_inc(s_w, 1)
            pool.wait_ge(s_idx, 1)
            pool.wait_ge(s_xnd, 64)

            def gather(j, k):
                pool.tensor_copy(gcol[:, k:k + 1], gidx[:, ds(j, 1)]).then_inc(s_gc, 1)
                hold(pool, s_gc, j + 1)
                pool.indirect_dma_start(xg[:, k, :], None, xn_dram,
                                        bass.IndirectOffsetOnAxis(gcol[:, k:k + 1], 0)).then_inc(s_gt[k], 16)

            def scatter(j, k):
                pool.wait_ge(s_y, j + 2)
                pool.tensor_copy(scol[:, k:k + 1], sidx[:, ds(j, 1)]).then_inc(s_sc, 1)
                hold(pool, s_sc, j + 1)
                pool.indirect_dma_start(y_dram, bass.IndirectOffsetOnAxis(scol[:, k:k + 1], 0),
                                        ysb[:, k, :], None).then_inc(s_st[k], 16)

            def split_due(before, j):
                done = pool.value_load(plan[0:1, ds(j + 1, 1)], min_val=0, max_val=PIECES * (E - 1))
                with pool.If(before < done):
                    with pool.Fori(before, done) as p:
                        part = pool.snap(p % PIECES * WP)
                        hold(pool, s_hi, p + (PIECES + 1))
                        lo, hi = (wslot(p // PIECES + 1, n, part) for n in (1, 0))
                        pool.tensor_tensor(lo, raw[:, ds(part, WP)], hi.bitcast(fp32), ALU.subtract).then_inc(s_w, 1)
                return done

            for j in range(DEEP):
                gather(j, j)
            for c in range(NCH):
                kb, l1, l3, _ = sets[c % 2]
                pool.wait_ge(s_c, c + 1)
                pool.tensor_tensor(kb, kb, l1, ALU.subtract).then_inc(s_u2, 1)
                pool.wait_ge(s_l3, c + 1)
                pool.wait_ge(s_l2, c + 1)
                pool.tensor_tensor(l3, l3, l2, ALU.subtract).then_inc(s_u1, 1)
                pool.wait_ge(s_u2, c + 1)
                pool.wait_ge(s_acp, c + 1)
                pool.tensor_tensor(kb.rearrange("p (q n) -> p q n", q=Q), kb.rearrange("p (q n) -> p q n", q=Q),
                                   A[:, :].rearrange("p (q n) -> p q n", q=Q)[:, :, c * CH:(c + 1) * CH],
                                   ALU.add).then_inc(s_u3, 1)
            pool.wait_ge(s_xt, 1)
            gather(DEEP, 0)
            pool.wait_ge(s_ctl, 1)
            split_due(0, 0)

            def body(i, hook=None):
                done = pool.value_load(plan[0:1, ds(LOOP * i + 1, 1)], min_val=0, max_val=PIECES * (E - 1))
                for u in range(LOOP):
                    j = LOOP * i + (1 + u)
                    pool.wait_ge(s_xt, j + 1)
                    gather(j + DEEP, (1 + u) % DEEP)
                    if hook:
                        hook(u)
                    scatter(j - 1, u)
                    done = split_due(done, j)

            def logh(g):
                pool.wait_ge(s_L, g + 1)
                pool.tensor_tensor(Ag[:, g, :], Ug[:, g, :], Ag[:, g, :], ALU.subtract).then_inc(s_lh, 1)

            with pool.Fori(0, 3) as i:
                body(i)
            body(3, logh)
            with pool.Fori(4, 9) as i:
                body(i)
            scatter(NTILES - 3, (NTILES - 3) % DEEP)
            split_due(pool.value_load(plan[0:1, NTILES - 2:NTILES - 1], min_val=0, max_val=PIECES * (E - 1)), NTILES - 2)
            scatter(NTILES - 2, (NTILES - 2) % DEEP)
            scatter(NTILES - 1, (NTILES - 1) % DEEP)
            for k in range(DEEP):
                pool.wait_ge(s_gt[k], 16 * len(range(k, LOOP * 9 + DEEP + 1, DEEP)))

        @block.scalar
        def _(act):
            n = [0]
            act.dma_start(small_sb[:, :], small).then_inc(s_small, 16)
            act.wait_ge(s_const, 14)
            for g in range(4):
                act.wait_ge(s_var0, g + 1)
                act.activation(std[:, 4 * g:4 * g + 4], mv[:, 4 * g:4 * g + 4, 1], ACT.Sqrt,
                               bias=eps[:, :]).then_inc(s_std0, 1)
            for m in range(NT // 2):
                act.wait_ge(s_xtr, m + 1)
                act.activation(xnT[:, :, 2 * P * m:2 * P * (m + 1)].rearrange("p q (t n) -> p t q n", t=2),
                               PS[:, (4 + m % 2) * 512:(5 + m % 2) * 512].rearrange("p (t q n) -> p t q n", t=2, q=Q),
                               ACT.Copy).then_inc(s_xnT, 1)
                if m == 1:
                    act.wait_ge(s_raw, LOADS)
                    for q in range(PIECES):
                        act.activation(wbuf[:, 0, 0, q * WP:(q + 1) * WP], raw[:, q * WP:(q + 1) * WP],
                                       ACT.Copy).then_inc(s_hi, 1)
            act.preload_act_table_set("natural_log_exp_and_others")
            act.wait_ge(s_u0i, 2)
            act.activation(u0t[:, 2, :], u0t[:, 0, :], ACT.Exp).then_inc(s_u0a, 1)
            act.activation(u0t[:, 3, :], u0t[:, 1, :], ACT.Ln, scale=2.0, bias=1.0).then_inc(s_u0b, 1)
            act.wait_ge(s_u0a, 1)
            act.activation(u0t[:, 4, :], u0t[:, 2, :], ACT.Ln, bias=1.0).then_inc(s_u0b, 1)
            act.wait_ge(s_nb, 1)

            def chunk(c):
                kb, l1, l3, nn = sets[c % 2]
                act.wait_ge(s_kp, c + 1)
                if c >= 2:
                    act.wait_ge(s_U, c - 1)
                if c == 1:
                    act.wait_ge(s_w, PIECES)
                for q in range(Q):
                    act.activation(kb[:, q * CH:(q + 1) * CH], k_ps[:, q * CH:(q + 1) * CH], ACT.Identity,
                                   bias=bias_sb[:, 0, q:q + 1]).then_inc(s_kb, 1)
                act.wait_ge(s_k, c + 1)
                for sign, dst, b in ((1.0, l3, bias_sb[:, 1, :]), (-1.0, nn, nbias[:, :])):
                    for q in range(Q):
                        act.activation(dst[:, q * CH:(q + 1) * CH], yh_ps[:, q * CH:(q + 1) * CH], ACT.Relu,
                                       scale=sign, bias=b[:, q:q + 1]).then_inc(s_yr, 1)
                act.wait_ge(s_kb, 2 * c + 2)
                act.activation(l1, kb, ACT.Abs).then_inc(s_e, 1)
                act.wait_ge(s_e, 3 * c + 1)
                act.activation(l1, l1, ACT.Exp, scale=-1.0).then_inc(s_e, 1)
                act.wait_ge(s_e, 3 * c + 2)
                act.activation(l1, l1, ACT.Ln, bias=1.0).then_inc(s_l1, 1)
                act.wait_ge(s_yr, 4 * c + 4)
                if c:
                    act.wait_ge(s_u1, c)
                act.activation(l2, nn, ACT.Exp, scale=-1.0).then_inc(s_e, 1)
                act.activation(l3, l3, ACT.Ln, scale=2.0, bias=1.0).then_inc(s_l3, 1)
                act.wait_ge(s_e, 3 * c + 3)
                act.activation(l2, l2, ACT.Ln, bias=1.0).then_inc(s_l2, 1)
                if c == 0:
                    act.wait_ge(s_zin, 1)
                    act.activation(w12[:, 1, :], w12[:, 0, :], ACT.Exp).then_inc(s_zex, 1)
            for c in range(NCH):
                chunk(c)

            def x_hi(j, slot):
                act.wait_ge(s_xt, j + 1)
                act.activation(xT[:, slot, 0, :], xT_ps, ACT.Copy).then_inc(s_xhi, 1)

            def h_hi(j):
                act.wait_ge(s_ht, j + 1)
                act.wait_ge(s_dn, j + 0)
                act.activation(hT[:, 0, :], hT_ps, ACT.Copy).then_inc(s_hhi, 1)

            def silu(j):
                act.wait_ge(s_up, j + 1)
                act.activation(sl, up_ps[:, 0:F], ACT.Silu).then_inc(s_silu, 1)

            def split_due(before, j):
                done = act.value_load(plan[0:1, ds(j + 1, 1)], min_val=0, max_val=PIECES * (E - 1))
                with act.If(before < done):
                    with act.Fori(before, done) as p:
                        part = act.snap(p % PIECES * WP)
                        hold(act, s_raw, p // PIECES * LOADS + 2 * LOADS)
                        act.activation(wslot(p // PIECES + 1, 0, part), raw[:, ds(part, WP)], ACT.Copy).then_inc(s_hi, 1)
                return done

            x_hi(0, 0)
            act.preload_act_table_set("silu_and_others")
            act.wait_ge(s_U, NCH)
            silu(0)
            x_hi(1, 1)
            act.wait_ge(s_ht, 1)
            act.activation(hT[:, 0, :], hT_ps, ACT.Copy).then_inc(s_hhi, 1)
            act.wait_ge(s_ctl, 1)
            split_due(0, 0)

            def body(i, steps=LOOP, hook=None):
                done = act.value_load(plan[0:1, ds(LOOP * i + 1, 1)], min_val=0, max_val=PIECES * (E - 1))
                for u in range(steps):
                    j = LOOP * i + (1 + u)
                    silu(j)
                    if steps == LOOP or u + 1 < steps:
                        x_hi(j + 1, u % 2)
                    if hook:
                        hook(u)
                    act.wait_ge(s_dn, j)
                    act.wait_ge(s_st[u], 16 * i + 16)
                    act.activation(ysb[:, u, :], y_ps, ACT.Copy).then_inc(s_y, 1)
                    h_hi(j)
                    if steps == LOOP or u + 1 < steps:
                        done = split_due(done, j)

            def h_copy(i, m0):
                def run(u):
                    m = LOOP * i + (u - m0)
                    act.wait_ge(s_htr, m + 1)
                    act.activation(hst[:, :, :], A[:, :].rearrange("p (q n) -> p q n", q=Q)[:, :, ds(m * 2 * P, 2 * P)],
                                   ACT.Copy).then_inc(s_h, 1)
                return run

            def x_again(i, m0):
                def run(u):
                    m = LOOP * i + (u - m0)
                    act.wait_ge(s_p2, 4 * m + 1)
                    act.dma_start(xre, x[ds(m * 2 * P, 2 * P), :].rearrange("(t p) d -> p t d", p=P)
                                  ).then_inc(s_xre, 16)
                return run
            with act.Fori(0, 2) as i:
                body(i)
            act.preload_act_table_set("natural_log_exp_and_others")
            for g in range(4):
                act.wait_ge(s_D, g + 1)
                act.activation(Dg[:, g, :], Dg[:, g, :], ACT.Exp).then_inc(s_De, 1)
                act.wait_ge(s_Em, g + 1)
                act.activation(Ug[:, g, :], Ug[:, g, :], ACT.Exp).then_inc(s_Ee, 1)
            act.preload_act_table_set("silu_and_others")
            body(2)
            act.preload_act_table_set("natural_log_exp_and_others")
            for g in range(4):
                act.wait_ge(s_S, g + 1)
                act.activation(Ug[:, g, :], Ug[:, g, :], ACT.Ln).then_inc(s_lS, 1)
            act.preload_act_table_set("silu_and_others")
            body(3)

            def finish(u):
                if u == 2:
                    act.wait_ge(s_var, 1)
                    act.activation(gs[:, 15:16], stat_ps[:, 2:3], ACT.Sqrt, scale=1.0 / (NSTAT - 1)).then_inc(s_std, 1)
                    act.preload_act_table_set("silu_and_others")
            body(4, hook=finish)
            act.preload_act_table_set("natural_log_exp_and_others")
            act.wait_ge(s_norm, 1)
            for g in range(4):
                act.activation(Ag[:, g, :], Ag[:, g, :], ACT.Exp, scale=gs[:, 8:9], bias=gs[:, 9:10]).then_inc(s_hx, 1)
            act.preload_act_table_set("silu_and_others")
            act.wait_ge(s_hx, 4)
            with act.Fori(5, 7) as i:
                body(i, hook=h_copy(i, LOOP * 5))
            act.wait_ge(s_p1, 4 * NT // 2 + 1)
            act.activation(std[:, :], mv[:, :, 1], ACT.Sqrt, bias=eps[:, :]).then_inc(s_std3, 1)
            act.preload_act_table_set("silu_and_others")
            with act.Fori(7, 9) as i:
                body(i, hook=x_again(i, LOOP * 7))
            body(9, NTILES - 1 - LOOP * 9)
            act.wait_ge(s_dn, NTILES)
            act.wait_ge(s_st[(NTILES - 1) % DEEP], 16 * (NTILES // DEEP + 1))
            act.activation(ysb[:, (NTILES - 1) % DEEP, :], y_ps, ACT.Copy).then_inc(s_y, 1)

        @block.vector
        def _(dve):
            n = [0]

            def step(ins):
                n[0] += 1
                ins.then_inc(s_dve, 1)
                dve.wait_ge(s_dve, n[0])

            dve.sem_inc(s_y, 1)
            dve.sem_inc(s_htr, 1)
            dve.sem_inc(s_p1, 1)
            dve.sem_inc(s_p2, 1)
            dve.memset(one8, 1.0)
            dve.memset(keep.rearrange("p (e t) -> p e t", e=E)[:, :, 1:NT], 1.0)
            dve.memset(keep.rearrange("p (e t) -> p e t", e=E)[:, :, 0:1], 0.0)
            def stats(g):
                dve.wait_ge(s_x[g], 16)
                for t in range(4 * g, 4 * g + 4):
                    ins = dve.bn_stats(bst[:, t, :], xn[:, t, :])
                step(ins)
                for t in range(4 * g, 4 * g + 4):
                    ins = dve.bn_aggr(mv[:, t, :], bst[:, t, :])
                ins.then_inc(s_var0, 1)

            stats(0)
            for g in range(4):
                if g < 3:
                    stats(g + 1)
                group = slice(4 * g, 4 * g + 4)
                dve.wait_ge(s_std0, g + 1)
                step(dve.reciprocal(rstd[:, group], std[:, group]))
                dve.scalar_tensor_tensor(nmean[:, group], mv[:, group, 0], -1.0, rstd[:, group], ALU.mult,
                                         ALU.mult).then_inc(s_mr, 1)
            dve.wait_ge(s_small, 16)
            dve.tensor_scalar(u0t[:, 0, :], h0_sb, 0.0, None, ALU.min).then_inc(s_u0i, 1)
            dve.tensor_scalar(u0t[:, 1, :], h0_sb, 0.0, None, ALU.max).then_inc(s_u0i, 1)
            dve.tensor_scalar(nbias[:, :], bias_sb[:, 1, :], -1.0, None, ALU.mult).then_inc(s_nb, 1)
            dve.wait_ge(s_lg, 1)

            def te(v):
                return v.rearrange("p (t e) -> p t e", e=E)

            def over_e(v):
                return v.rearrange("p (t a) -> p t a", a=1).to_broadcast([P, NT, E])
            ramp = iota_c[:, 0:E].rearrange("p (a e) -> p a e", a=1).to_broadcast([P, NT, E])
            step(dve.tensor_copy(logit, logit_ps))
            m1, m2 = m12[:, 0:NT], m12[:, NT:2 * NT]
            for mx, src, hot in ((m1, logit, hot1), (m2, t_b, hot2)):
                step(dve.tensor_reduce(mx, te(src), AX.X, ALU.max))
                step(dve.tensor_tensor(te(t_a), te(src), over_e(mx), ALU.is_equal))
                step(dve.scalar_tensor_tensor(te(t_a), ramp, float(P), te(t_a), ALU.subtract, ALU.mult))
                step(dve.tensor_reduce(idx8, te(t_a), AX.X, ALU.min))
                step(dve.scalar_tensor_tensor(te(hot), ramp, float(P), over_e(idx8), ALU.subtract, ALU.is_equal))
                if hot is hot1:
                    step(dve.scalar_tensor_tensor(t_b, hot1, -BIG, logit, ALU.mult, ALU.add))
            dve.tensor_tensor(w12[:, 0, :], m2, m1, ALU.subtract).then_inc(s_zin, 1)
            step(dve.tensor_tensor(pick, hot1, hot2, ALU.add))
            dve.tensor_copy(pick_b[:, :], pick).then_inc(s_pick, 1)
            dve.wait_ge(s_rank, 1)
            et = "p (e t) -> p e t"
            step(dve.tensor_copy(tot.rearrange(et, e=E), tot_ps.rearrange("p (t e) -> p e t", e=E)))
            step(dve.tensor_tensor_scan(cum, keep, tot, 0.0, ALU.mult, ALU.add))
            step(dve.tensor_copy(cnt, cum.rearrange(et, e=E)[:, :, NT - 1]))
            step(dve.tensor_scalar(eid_f[:, 0:NT], iota_c[:, 0:NT], float(P), None, ALU.mult))
            step(dve.tensor_tensor(thr.rearrange(et, e=E), cnt.rearrange("p (e a) -> p e a", a=1).to_broadcast([P, E, NT]),
                                   eid_f[:, 0:NT].rearrange("p (a t) -> p a t", a=1).to_broadcast([P, E, NT]), ALU.is_gt))
            step(dve.tensor_reduce(ntile, thr.rearrange(et, e=E), AX.X, ALU.add))
            step(dve.tensor_scalar(ntile, ntile, 1.0, None, ALU.max))
            step(dve.tensor_tensor_scan(tend, one8, ntile, 0.0, ALU.mult, ALU.add))
            step(dve.tensor_tensor(tstart, tend, ntile, ALU.subtract))
            step(dve.tensor_tensor(cum, cum, tot, ALU.subtract))
            step(dve.scalar_tensor_tensor(cum.rearrange(et, e=E), tstart.rearrange("p (e a) -> p e a", a=1)
                                          .to_broadcast([P, E, NT]), float(P), cum.rearrange(et, e=E), ALU.mult, ALU.add))
            step(dve.tensor_tensor(te(slots), cum.rearrange("p (e t) -> p t e", e=E), te(rank_ps), ALU.add))
            for k, hot in ((0, hot1), (1, hot2)):
                step(dve.tensor_tensor(t_a, hot, slots, ALU.mult))
                step(dve.tensor_reduce(slot_f[:, k * NT:(k + 1) * NT], te(t_a), AX.X, ALU.add))
            step(dve.tensor_copy(slot_i[:, 0, :], slot_f))
            step(dve.tensor_scalar(slot_i[:, 1, :], slot_i[:, 0, :], P - 1, None, ALU.bitwise_and))
            step(dve.tensor_scalar(slot_i[:, 2, :], slot_i[:, 0, :], 7, None, ALU.logical_shift_right))
            step(dve.tensor_copy(pos_f, slot_i[:, 1, :]))
            step(dve.tensor_copy(tile_f, slot_i[:, 2, :]))
            oh = onehot_tile.rearrange("p (s c) -> p s c", c=NCOL)
            step(dve.tensor_tensor(oh, iota_c[:, 0:NCOL].rearrange("p (a c) -> p a c", a=1).to_broadcast([P, 2 * NT, NCOL]),
                                   tile_f.rearrange("p (s a) -> p s a", a=1).to_broadcast([P, 2 * NT, NCOL]), ALU.is_equal))
            step(dve.tensor_tensor(oh, oh.bitcast(fp32), id_f.rearrange("p (s a) -> p s a", a=1)
                                   .to_broadcast([P, 2 * NT, NCOL]), ALU.mult))
            def softplus(c):
                kb, l1, _, _ = sets[c % 2]
                dve.wait_ge(s_l1, c + 1)
                dve.wait_ge(s_kb, 2 * c + 2)
                dve.scalar_tensor_tensor(l1, kb, 0.0, l1, ALU.max, ALU.add).then_inc(s_c, 1)

            def a_copy(c):
                dve.wait_ge(s_cum, c + 1)
                dve.tensor_copy(A[:, :].rearrange("p (q n) -> p q n", q=Q)[:, :, c * CH:(c + 1) * CH],
                                cum_ps.rearrange("p (q n) -> p q n", q=Q)).then_inc(s_acp, 1)

            def log_values(c):
                kb, _, l3, nn = sets[c % 2]
                dve.wait_ge(s_u1, c + 1)
                dve.wait_ge(s_yr, 4 * c + 4)
                dve.tensor_tensor(l3, l3, nn, ALU.subtract).then_inc(s_ua, 1)
                dve.wait_ge(s_ua, c + 1)
                dve.wait_ge(s_u3, c + 1)
                dve.tensor_tensor(U[:, :].rearrange("p (q n) -> p q n", q=Q)[:, :, c * CH:(c + 1) * CH],
                                  l3.rearrange("p (q n) -> p q n", q=Q), kb.rearrange("p (q n) -> p q n", q=Q),
                                  ALU.add).then_inc(s_U, 1)

            softplus(0)
            for m in range(2 * NT // 4):
                if m >= 2:
                    dve.wait_ge(s_posu, m - 1)
                dve.tensor_tensor(onehot_pos[:, m % 2, :].rearrange("p (s c) -> p s c", c=P),
                                  iota_c[:, :].rearrange("p (a c) -> p a c", a=1).to_broadcast([P, 4, P]),
                                  pos_f[:, 4 * m:4 * m + 4].rearrange("p (s a) -> p s a", a=1).to_broadcast([P, 4, P]),
                                  ALU.is_equal).then_inc(s_pos, 1)
            dve.wait_ge(s_posu, 2 * NT // 4)
            step(dve.tensor_copy(dtab, table_ps))
            step(dve.scalar_tensor_tensor(dpad, dtab, 0.0, pad_row, ALU.is_equal, ALU.mult))
            step(dve.tensor_scalar(dtab, dtab, -1.0, None, ALU.add))
            step(dve.tensor_scalar(dtok, dtab, float(NTOK), float(-NTOK), ALU.is_ge, ALU.mult))
            step(dve.tensor_tensor(dtok, dtok, dtab, ALU.add))
            step(dve.tensor_scalar(gidx[:, :], dtok, 0.0, None, ALU.max))
            step(dve.tensor_tensor(dpad, dpad, dtab, ALU.add))
            dve.tensor_copy(sidx[:, :], dpad).then_inc(s_idx, 1)
            dve.wait_ge(s_idx, 1)
            dve.wait_ge(s_zex, 1)
            step(dve.tensor_scalar(w12[:, 0, :], w12[:, 1, :], 1.0, None, ALU.add))
            step(dve.reciprocal(w12[:, 0, :], w12[:, 0, :]))
            step(dve.tensor_tensor(w12[:, 1, :], w12[:, 1, :], w12[:, 0, :], ALU.mult))
            dve.wait_ge(s_u0b, 2)
            step(dve.tensor_tensor(u0t[:, 5, :], u0t[:, 3, :], u0t[:, 4, :], ALU.subtract))
            for b in range(B):
                step(dve.tensor_tensor(u0[:, :].rearrange("p (q b) -> p q b", b=B)[:, :, b], u0t[:, 5, :],
                                       u0t[:, 0, :], ALU.add))

            def tile_plan():
                c8 = cmp8.rearrange("p (c e) -> p c e", e=E)
                cols = iota_c[:, 0:NCOL].rearrange("p (c a) -> p c a", a=1)
                step(dve.tensor_tensor(c8, tend.rearrange("p (a e) -> p a e", a=1).to_broadcast([P, NCOL, E]),
                                       cols.to_broadcast([P, NCOL, E]), ALU.is_le))
                step(dve.tensor_reduce(eid_f, c8, AX.X, ALU.add))
                step(dve.tensor_scalar(eid_f, eid_f, float(E - 1), None, ALU.min))
                step(dve.tensor_copy(eid[:, :], eid_f))
                step(dve.tensor_scalar(last, tend, -1.0, None, ALU.add))
                step(dve.memset(plan_f, 0.0))
                n_at = len(AT) - 1
                when3 = when.rearrange("p (a e) -> p a e", a=n_at)
                for k, at in enumerate(AT[1:]):
                    dve.tensor_scalar(when3[:, k, 1:], tstart[:, 1:E - 1], float(at), None, ALU.add)
                    ins = dve.tensor_scalar(when3[:, k, 0:1], tstart[:, 0:1], float(at + 1), None, ALU.add)
                step(ins)
                step(dve.tensor_tensor(when3, when3, last[:, 0:E - 1].rearrange("p (a e) -> p a e", a=1)
                                       .to_broadcast([P, n_at, E - 1]), ALU.min))
                was = due.rearrange("p (c w) -> p c w", c=NCOL)
                step(dve.tensor_tensor(was, when.rearrange("p (a w) -> p a w", a=1)
                                       .to_broadcast([P, NCOL, n_at * (E - 1)]),
                                       cols.to_broadcast([P, NCOL, n_at * (E - 1)]), ALU.is_le))
                step(dve.tensor_reduce(plan_f[:, 1:NCOL + 1], was, AX.X, ALU.add))
                step(dve.tensor_reduce(eid_f, was[:, :, 0:E - 1], AX.X, ALU.add))
                step(dve.tensor_tensor(plan_f[:, 1:NCOL + 1], eid_f, plan_f[:, 1:NCOL + 1], ALU.add))
                dve.tensor_copy(plan[:, :], plan_f).then_inc(s_ctl, 1)
                dve.wait_ge(s_ctl, 1)

            for c in range(NCH):
                if c:
                    softplus(c)
                    log_values(c - 1)
                a_copy(c)
                if c == 1:
                    tile_plan()
            log_values(NCH - 1)

            def x_lo(j, slot):
                dve.wait_ge(s_xhi, j + 1)
                dve.tensor_tensor(xT[:, slot, 1, :], xT_ps, xT[:, slot, 0, :].bitcast(fp32),
                                  ALU.subtract).then_inc(s_xlo, 1)

            def h_lo(j):
                dve.wait_ge(s_hhi, j + 1)
                dve.tensor_tensor(hT[:, 1, :], hT_ps, hT[:, 0, :].bitcast(fp32), ALU.subtract).then_inc(s_hlo, 1)

            def gate(j):
                dve.wait_ge(s_silu, j + 1)
                dve.tensor_tensor(g_h, sl, up_ps[:, F:2 * F], ALU.mult).then_inc(s_g, 1)

            x_lo(0, 0)
            gate(0)
            x_lo(1, 1)
            h_lo(0)
            dve.wait_ge(s_k, NCH)
            step(dve.tensor_copy(M[:, :, 0], u0[:, :]))

            def body(i, steps=LOOP, hook=None):
                for u in range(steps):
                    j = LOOP * i + (1 + u)
                    dve.wait_ge(s_ht, j)
                    gate(j)
                    if steps == LOOP or u + 1 < steps:
                        x_lo(j + 1, u % 2)
                    h_lo(j)
                    if hook:
                        hook(u)

            def run_max(g):
                dve.tensor_tensor_scan(M[:, g, 1:T + 1], Ug[:, g, :], Ug[:, g, :], u0[:, g:g + 1],
                                       ALU.max, ALU.max).then_inc(s_M, 1)
                dve.wait_ge(s_M, g + 1)
                dve.tensor_tensor(Dg[:, g, :], M[:, g, 0:T], M[:, g, 1:T + 1], ALU.subtract).then_inc(s_D, 1)

            def less_max(g):
                dve.tensor_tensor(Ug[:, g, :], Ug[:, g, :], M[:, g, 1:T + 1], ALU.subtract).then_inc(s_Em, 1)

            def run_scan(g):
                dve.wait_ge(s_De, g + 1)
                dve.wait_ge(s_Ee, g + 1)
                dve.tensor_tensor_scan(Ug[:, g, :], Dg[:, g, :], Ug[:, g, :], 1.0, ALU.mult,
                                       ALU.add).then_inc(s_S, 1)

            def plus_max(g):
                dve.wait_ge(s_lS, g + 1)
                dve.tensor_tensor(Ug[:, g, :], Ug[:, g, :], M[:, g, 1:T + 1], ALU.add).then_inc(s_L, 1)

            def sums():
                dve.wait_ge(s_lh, 4)
                for m in range(8):
                    ins = dve.bn_stats(gst[:, m, :], A[:, 512 * m:512 * (m + 1)])
                step(ins)
                step(dve.bn_aggr(gs[:, 0:2], gst[:, :, :].rearrange("p a b -> p (a b)")))
                step(dve.tensor_reduce(gs[:, 2:3], u0[:, :], AX.X, ALU.add))
                dve.scalar_tensor_tensor(gs[:, 3:4], gs[:, 0:1], float(2 * NTOK), gs[:, 2:3], ALU.mult,
                                         ALU.add).then_inc(s_mean_in, 1)

            def squares():
                dve.wait_ge(s_mean, 1)
                step(dve.tensor_scalar(gs[:, 4:5], stat_ps[:, 0:1], 1.0 / NSTAT, None, ALU.mult))
                step(dve.tensor_scalar(gs[:, 5:6], gs[:, 0:1], gs[:, 4:5], None, ALU.subtract))
                step(dve.scalar_tensor_tensor(gs[:, 6:7], gs[:, 5:6], gs[:, 5:6], gs[:, 1:2], ALU.mult, ALU.add))
                step(dve.tensor_scalar(gs[:, 10:14], u0[:, :], gs[:, 4:5], None, ALU.subtract))
                step(dve.tensor_tensor(gs[:, 10:14], gs[:, 10:14], gs[:, 10:14], ALU.mult))
                step(dve.tensor_reduce(gs[:, 14:15], gs[:, 10:14], AX.X, ALU.add))
                dve.scalar_tensor_tensor(gs[:, 7:8], gs[:, 6:7], float(2 * NTOK), gs[:, 14:15], ALU.mult,
                                         ALU.add).then_inc(s_var_in, 1)

            def normaliser():
                dve.wait_ge(s_std, 1)
                step(dve.reciprocal(gs[:, 8:9], gs[:, 15:16]))
                step(dve.scalar_tensor_tensor(gs[:, 9:10], gs[:, 4:5], -1.0, gs[:, 8:9], ALU.mult, ALU.mult))
                dve.sem_inc(s_norm, 1)

            def row_stats(i, m0):
                def run(u):
                    m = LOOP * i + (u - m0)
                    rows = xn[:, ds(2 * m, 2), :]
                    dve.wait_ge(s_htr, m + 2)
                    dve.tensor_tensor(rtmp, tr_ps.rearrange("p (t d) -> p t d", t=2), rows, ALU.add).then_inc(s_p1, 1)
                    hold(dve, s_p1, 4 * m + 2)
                    dve.tensor_copy(rows, rtmp)
                    for t in range(2):
                        ins = dve.bn_stats(st3[:, t, :], rtmp[:, t, :])
                    ins.then_inc(s_p1, 1)
                    hold(dve, s_p1, 4 * m + 3)
                    for t in range(2):
                        ins = dve.bn_aggr(mv3[:, t, :], st3[:, t, :])
                    ins.then_inc(s_p1, 1)
                    dve.wait_ge(s_p1, 4 * m + 4)
                    dve.tensor_copy(mv[:, ds(2 * m, 2), :], mv3[:, :, :]).then_inc(s_p1, 1)
                return run

            def last_norm(i, m0):
                def run(u):
                    m = LOOP * i + (u - m0)
                    rows = xn[:, ds(2 * m, 2), :]
                    for t in range(2):
                        row = xn[:, ds(2 * m + t, 1), :].rearrange("p a d -> p (a d)")
                        ins = dve.tensor_scalar(row, row, mv[:, ds(2 * m + t, 1), 0:1].rearrange("p a b -> p (a b)"),
                                                rstd[:, ds(2 * m + t, 1)], ALU.subtract, ALU.mult)
                    ins.then_inc(s_p2, 1)
                    dve.wait_ge(s_p2, 4 * m + 2)
                    for k in range(2):
                        dve.tensor_tensor(rows, rows, lnwb[:, k:k + 1, :].to_broadcast([P, 2, D]),
                                          ALU.add if k else ALU.mult).then_inc(s_p2, 1)
                        dve.wait_ge(s_p2, 4 * m + (3 + k))
                    dve.wait_ge(s_xre, 16 * m + 16)
                    dve.tensor_tensor(rows, rows, xre, ALU.add).then_inc(s_p2, 1)
                return run

            def global_stats(u):
                if u < 3:
                    (sums, squares, normaliser)[u]()
            for i, hook in enumerate((run_max, less_max, run_scan, plus_max, global_stats)):
                body(i, hook=hook)
            with dve.Fori(5, 7) as i:
                body(i, hook=row_stats(i, LOOP * 5))
            dve.wait_ge(s_std3, 1)
            step(dve.reciprocal(rstd[:, :], std[:, :]))
            with dve.Fori(7, 9) as i:
                body(i, hook=last_norm(i, LOOP * 7))
            body(9, NTILES - 1 - LOOP * 9)
            for g in range(4):
                dve.wait_ge(s_yl[g], 32)
                for t in range(4 * g, 4 * g + 4):
                    ins = dve.scalar_tensor_tensor(xn[:, t, :], U[:, D * t:D * (t + 1)], w12[:, 0, t:t + 1],
                                                   xn[:, t, :], ALU.mult, ALU.add)
                step(ins)
                for t in range(4 * g, 4 * g + 4):
                    ins = dve.scalar_tensor_tensor(xn[:, t, :], A[:, D * t:D * (t + 1)], w12[:, 1, t:t + 1],
                                                   xn[:, t, :], ALU.mult, ALU.add)
                ins.then_inc(s_fin, 1)

        @block.tensor
        def _(pe):
            pe.wait_ge(s_const, 14)
            pe.wait_ge(s_small, 16)
            for m in range(NT // 2):
                pe.wait_ge(s_xn, m // 2 + 1)
                if m >= 2:
                    pe.wait_ge(s_xnT, m - 1)
                for t in range(2):
                    for q in range(Q):
                        col = (4 + m % 2) * 512 + (t * Q + q) * P
                        ins = pe.transpose(PS[:, col:col + P], xn[:, 2 * m + t, q * P:(q + 1) * P], ident[:, :])
                ins.then_inc(s_xtr, 1)
                for k in (m - 1, m) if m == NT // 2 - 1 else (m - 1,) if m else ():
                    pe.wait_ge(s_xnT, k + 1)
                    for t in (2 * k, 2 * k + 1):
                        for q in range(Q):
                            ins = pe.matmul(logit_ps[:, t * E:(t + 1) * E], xnT[:, q, t * P:(t + 1) * P],
                                            wg_sb[:, q, :], start=(q == 0), stop=(q == Q - 1))
            ins.then_inc(s_lg, 1)

            def project(c, between=None):
                for mat, base in ((0, 0), (1, 2 * CH)):
                    if c and mat == 0:
                        pe.wait_ge(s_kb, 2 * c)
                    if c and mat == 1:
                        pe.wait_ge(s_yr, 4 * c)
                    for qo in range(Q):
                        for q in range(Q):
                            ins = pe.matmul(PS[:, base + qo * CH:base + (qo + 1) * CH],
                                            wzh_sb[:, q, mat, qo * P:(qo + 1) * P], xnT[:, q, c * CH:(c + 1) * CH],
                                            start=(q == 0), stop=(q == Q - 1))
                    ins.then_inc(s_k if mat else s_kp, 1)
                    if between and mat == 0:
                        between()

            def cumsum(c):
                pe.wait_ge(s_c, c + 1)
                l1 = sets[c % 2][1]
                if c:
                    pe.wait_ge(s_acp, c)
                pe.matmul(cum_ps[:, 0:CH], tri[:, :], l1[:, 0:CH], start=True, stop=True)
                pe.matmul(cum_ps[:, CH:2 * CH], ones[:, :], l1[:, 0:CH], start=True, stop=False)
                pe.matmul(cum_ps[:, CH:2 * CH], tri[:, :], l1[:, CH:2 * CH], start=False,
                          stop=True).then_inc(s_cum, 1)
            def ranks():
                pe.wait_ge(s_pick, 1)
                pe.matmul(rank_ps, tri_b[:, :], pick_b[:, :], start=True, stop=True)
                pe.matmul(tot_ps, ones_b[:, :], pick_b[:, :], start=True, stop=True).then_inc(s_rank, 1)
            project(0, ranks)
            project(1)
            for m in range(2 * NT // 4):
                pe.wait_ge(s_pos, m + 1)
                for s in range(4):
                    r = 4 * m + s
                    ins = pe.matmul(table_ps, onehot_pos[:, m % 2, s * P:(s + 1) * P],
                                    onehot_tile[:, r * NCOL:(r + 1) * NCOL], start=(r == 0), stop=(r == 2 * NT - 1))
                ins.then_inc(s_posu, 1)
            cumsum(0)
            for c in range(1, NCH):
                if c + 1 < NCH:
                    project(c + 1)
                cumsum(c)

            def x_tile(j, k, val):
                pe.wait_ge(s_gt[k], val)
                for q in range(Q):
                    ins = pe.transpose(xT_ps[:, q * P:(q + 1) * P], xg[:, k, q * P:(q + 1) * P], ident[:, :])
                ins.then_inc(s_xt, 1)

            def either(e, products):
                if isinstance(e, int):
                    products(e % 2)
                    return
                with pe.If(e % 2 > 0):
                    products(1)
                with pe.Else():
                    products(0)

            def up(j, slot, e):
                pe.wait_ge(s_xlo, j + 1)
                hold(pe, s_w, PIECES * e + (PIECES - 1))

                def products(w):
                    for q in range(Q):
                        for xpart, wpart in ((0, 0), (0, 1), (1, 0)):
                            for a, b in UP_PIECES:
                                ins = pe.matmul(up_ps[:, a:b], xT[:, slot, xpart, q * P:(q + 1) * P],
                                                wbuf[:, w, wpart, q * 2 * F + a:q * 2 * F + b],
                                                start=(q == 0 and xpart == 0 and wpart == 0),
                                                stop=(q == Q - 1 and xpart == 1))
                    ins.then_inc(s_up, 1)
                either(e, products)

            def down(j, e):
                pe.wait_ge(s_w, PIECES * e + PIECES)
                pe.wait_ge(s_y, j + 1)
                hold(pe, s_hlo, j + 1)

                def products(w):
                    for c in range(HC):
                        for hpart, wpart in ((0, 0), (0, 1), (1, 0)):
                            ins = pe.matmul(y_ps, hT[:, hpart, c * P:(c + 1) * P],
                                            wbuf[:, w, wpart, W13 + c * D:W13 + (c + 1) * D],
                                            start=(c == 0 and hpart == 0 and wpart == 0),
                                            stop=(c == HC - 1 and hpart == 1))
                    ins.then_inc(s_dn, 1)
                either(e, products)

            def h_tile(j):
                pe.wait_ge(s_g, j + 1)
                for c in range(HC):
                    a = min(c * P, F - P)
                    ins = pe.transpose(hT_ps[:, c * P:(c + 1) * P], g_h[:, a:a + P], ident[:, :])
                ins.then_inc(s_ht, 1)

            pe.wait_ge(s_acp, NCH)
            pe.wait_ge(s_kb, 2 * NCH)
            pe.wait_ge(s_yr, 4 * NCH)
            x_tile(0, 0, 16)
            up(0, 0, 0)
            x_tile(1, 1, 16)
            h_tile(0)
            pe.wait_ge(s_ctl, 1)

            def body(i, steps=LOOP, hook=None):
                def expert(k):
                    return pe.value_load(eid[0:1, ds(LOOP * i + k, 1)], min_val=0, max_val=E - 1)
                before, e = expert(0), expert(1)
                for u in range(steps):
                    j = LOOP * i + (1 + u)
                    pe.wait_ge(s_g, j)
                    up(j, (1 + u) % 2, e)
                    if steps == LOOP or u + 1 < steps:
                        x_tile(j + 1, (2 + u) % DEEP, 16 * i + 16 * ((2 + u) // DEEP + 1))
                    down(j - 1, before)
                    before = e
                    if u + 1 < steps:
                        e = expert(u + 2)
                    h_tile(j)
                    if hook:
                        hook(u)

            def sum_all(src, col, s_in, s_out):
                pe.wait_ge(s_in, 1)
                pe.matmul(stat_ps[:, col:col + 1], ones[:, :], src, start=True, stop=True).then_inc(s_out, 1)

            def h_back(i, m0):
                def run(u):
                    m = LOOP * i + (u - m0)
                    pe.wait_ge(s_h, m + 1)
                    pe.wait_ge(s_p1, 4 * m + 1)
                    for t in range(2):
                        for q in range(Q):
                            col = (t * Q + q) * P
                            ins = pe.transpose(tr_ps[:, col:col + P], hst[:, q, t * P:(t + 1) * P], ident[:, :])
                    ins.then_inc(s_htr, 1)
                return run

            def global_stats(u):
                if u == 1:
                    sum_all(gs[:, 3:4], 0, s_mean_in, s_mean)
                if u == 2:
                    sum_all(gs[:, 7:8], 2, s_var_in, s_var)
            with pe.Fori(0, 4) as i:
                body(i)
            body(4, hook=global_stats)
            with pe.Fori(5, 7) as i:
                body(i, hook=h_back(i, LOOP * 5))
            with pe.Fori(7, 9) as i:
                body(i)
            body(9, NTILES - 1 - LOOP * 9)
            e = pe.value_load(eid[0:1, NTILES - 1:NTILES], min_val=0, max_val=E - 1)
            down(NTILES - 1, e)




def kernel(**inputs):
    import numpy as _np
    import concourse.bacc as _bacc
    from concourse import mybir as _mybir
    from concourse.bass_utils import run_bass_kernel_spmd as _run

    a = {k: _np.ascontiguousarray(v) for k, v in inputs.items()}
    w1, w2, w3 = a["L0_ffn_w1"], a["L0_ffn_w2"], a["L0_ffn_w3"]
    up = _np.concatenate([w1, w3], 1).transpose(0, 2, 1).reshape(E, Q, P, 2 * F).transpose(0, 2, 1, 3)
    dn = w2.transpose(0, 2, 1)
    main = _np.concatenate([up.reshape(E, P, W13),
                            dn[:, 0:FULL * P].reshape(E, FULL, P, D).transpose(0, 2, 1, 3).reshape(E, P, FULL * D)], 2)
    zh = _np.stack([a["L0_attn_W_z"].T, a["L0_attn_W_h"].T], 1)
    small = {
        "wzh": zh.reshape(Q, P, 2, D).transpose(1, 0, 2, 3),
        "wg": a["L0_ffn_w_gate"].T.reshape(Q, P, E).transpose(1, 0, 2),
        "bias": _np.stack([a["L0_attn_b_z"], a["L0_attn_b_h"]]).reshape(2, Q, P).transpose(2, 0, 1),
        "h0": a["L0_attn_h0"].reshape(Q, P).T,
        "ln": _np.stack([a["L0_attn_ln_w"], a["L0_attn_ln_b"]])[None].repeat(P, 0),
    }
    arrays = {
        "x": a["L0_attn_hidden_states"].reshape(NTOK, D),
        "small": _np.concatenate([small[name].reshape(P, n) for name, n in SMALL], 1),
        "w_main": main,
        "w_tail": dn[:, FULL * P:],
    }
    arrays = {k: _np.ascontiguousarray(v) for k, v in arrays.items()}
    nc = _bacc.Bacc("TRN2", target_bir_lowering=False, num_devices=1)
    f32 = _mybir.dt.float32
    args = [nc.dram_tensor(n, v.shape, f32, kind="ExternalInput").ap() for n, v in arrays.items()]
    args.append(nc.dram_tensor("out", [NTOK, D], f32, kind="ExternalOutput").ap())
    args.append(nc.dram_tensor("xn_dram", [NTOK, D], f32).ap())
    args.append(nc.dram_tensor("y_dram", [2 * NTOK + 2 * DEEP * P, D], f32).ap())
    build_program(nc, *args)
    r = _run(nc, [arrays], core_ids=[0])
    return r.results[0]["out"].reshape(B, T, D)
```

```python
import concourse.bass as bass
from concourse import mybir
from contextlib import ExitStack

P = 128
B, T, D = 2, 1024, 256
NTOK = B * T
NT = NTOK // P
Q = D // P
E, F = 8, 704
NTILES = (2 * NTOK + E * (P - 1)) // P
ORDER = (0, 2, 1, 3)
AT = (0, 0, 1, 2)
DEEP = 4
NCOL = -(-NTILES // DEEP) * DEEP + DEEP
LOOP = 4
SURE = 2 * NTOK // P + 1
FULL = F // P
HC = FULL + 1
TAIL = F - FULL * P
W13 = Q * 2 * F
WMAIN = W13 + FULL * D
WALL = WMAIN + D
LOADS = 5 * 16
PIECES = 4
WP = WALL // PIECES
SMALL = [("wzh", Q * 2 * D), ("wg", Q * E), ("bias", 2 * Q), ("h0", Q), ("ln", 2 * D)]
CH = 512
NCH = NTOK // CH
LN_EPS = 1e-5
NSTAT = B * (T + 1) * D
SCRATCH = 2 * NTOK
UP_PIECES = [(0, 512), (512, 1024), (1024, 1408)]
BIG = 3.0e38


def build_program(nc, x, small, w_main, w_tail, out, xn_dram, y_dram):
    fp32, f32r, i32 = mybir.dt.float32, mybir.dt.float32r, mybir.dt.int32
    u32, bf16 = mybir.dt.uint32, mybir.dt.bfloat16
    ALU, ACT, AX = mybir.AluOpType, mybir.ActivationFunctionType, mybir.AxisListType
    ds = bass.ds
    ctx = ExitStack()
    with ctx:
        def sb(name, shape, dt=fp32):
            return ctx.enter_context(nc.sbuf_tensor(name, shape, dt))

        def sem(name):
            return ctx.enter_context(nc.semaphore(name))

        xn = sb("xn", [P, NT, D])
        xnT_M = sb("xnT_M", [P, 2 * NTOK])
        xnT = xnT_M[:, :].rearrange("p (q n) -> p q n", q=Q)
        M = xnT_M[:, :].rearrange("p (g t) -> p g t", g=4)
        U = sb("U", [P, 2 * NTOK])
        Ug = U[:, :].rearrange("p (g t) -> p g t", g=4)
        A = sb("A", [P, 2 * NTOK])
        Ag = A[:, :].rearrange("p (g t) -> p g t", g=4)
        wbuf = sb("wbuf", [P, 2, 2, WALL], f32r)
        wflat = wbuf[:, :, :, :].rearrange("p s h n -> p (s h n)")
        raw = sb("raw", [P, WALL])
        tmp = sb("tmp", [P, 6, Q * CH])
        tflat = tmp[:, :, :].rearrange("p a n -> p (a n)")
        l2s = [tmp[:, 4, :], tmp[:, 5, :]]
        sets = [[tmp[:, n, :] for n in range(4)], [raw[:, n * Q * CH:(n + 1) * Q * CH] for n in range(4)]]
        g_h = tflat[:, 0:F]
        sl = tflat[:, F:2 * F]
        Dg = tmp[:, 2:6, :]
        rtmp, xre = (tmp[:, 5, k * 2 * D:(k + 1) * 2 * D].rearrange("p (t d) -> p t d", t=2) for k in range(2))
        hst = sb("hst", [P, Q, 2 * P])
        eps = sb("eps", [P, 1])
        hT = sb("hT", [P, 2, HC * P], f32r)
        xT = sb("xT", [P, 2, 2, D], f32r)
        onehot_tile = hT[:, :, :].rearrange("p a n -> p (a n)")[:, 0:2 * NT * NCOL]
        onehot_pos = xT[:, :, :, :].rearrange("p a b n -> p a (b n)")
        work = sb("work", [P, 2 * DEEP * D])
        xg = work[:, 0:DEEP * D].rearrange("p (k d) -> p k d", d=D)
        ysb = work[:, DEEP * D:2 * DEEP * D].rearrange("p (k d) -> p k d", d=D)
        small_sb = sb("small_sb", [P, sum(n for _, n in SMALL)])
        where, start = {}, 0
        for name, n in SMALL:
            where[name] = small_sb[:, start:start + n]
            start += n
        wzh_sb = where["wzh"].rearrange("p (q m d) -> p q m d", q=Q, m=2)
        wg_sb = where["wg"].rearrange("p (q e) -> p q e", q=Q)
        bias_sb = where["bias"].rearrange("p (m q) -> p m q", m=2)
        h0_sb = where["h0"]
        lnwb = where["ln"].rearrange("p (m d) -> p m d", m=2)
        nbias = sb("nbias", [P, Q])
        nmean = sb("nmean", [P, NT])
        ident = sb("ident", [P, P])
        tri = sb("tri", [P, P])
        ones = sb("ones", [P, P])
        tri_b = sb("tri_b", [P, P], bf16)
        ones_b = sb("ones_b", [P, P], bf16)
        pick_b = sb("pick_b", [P, NT * E], bf16)
        iota_c = sb("iota_c", [P, P])
        bst = sb("bst", [P, NT, 6])
        mv = sb("mv", [P, NT, 2])
        rstd = sb("rstd", [P, NT])
        w12 = sb("w12", [P, 2, NT])
        slot_i = sb("slot_i", [P, 3, 2 * NT], i32)
        gcol = sb("gcol", [P, DEEP], u32)
        scol = sb("scol", [P, DEEP], u32)
        gidx = sb("gidx", [P, NCOL], u32)
        sidx = sb("sidx", [P, NCOL], u32)
        eid = sb("eid", [P, NCOL], i32)
        tiles = sb("tiles", [P, 1], i32)
        plan = sb("plan", [P, NCOL + 1], i32)
        u0 = sb("u0", [P, 4])
        u0t = sb("u0t", [P, 6, Q])
        gst = sb("gst", [P, 8, 6])
        gs = sb("gs", [P, 16])
        st3 = sb("st3", [P, 2, 6])
        mv3 = sb("mv3", [P, 2, 2])
        std = sb("std", [P, NT])
        at = [0]

        def ut(cols):
            at[0] += cols
            return work[:, at[0] - cols:at[0]]
        logit = ut(NT * E)
        t_a, t_b, hot1, hot2, pick, slots = (ut(NT * E) for _ in range(6))
        tot = ut(E * NT)
        cum = ut(E * NT)
        keep = ut(E * NT)
        m12 = ut(2 * NT)
        idx8 = ut(NT)
        slot_f, pos_f, tile_f, id_f = (ut(2 * NT) for _ in range(4))
        cnt, one8 = (ut(E) for _ in range(2))
        thr = ut(E * NT)
        dtab, dpad, dtok = (ut(NCOL) for _ in range(3))
        pad_row = ut(NCOL)
        hflat = hst[:, :, :].rearrange("p q n -> p (q n)")
        ht_at = [0]

        def pt(cols):
            ht_at[0] += cols
            return hflat[:, ht_at[0] - cols:ht_at[0]]
        cmp8 = pt(NCOL * E)
        ntile, tend, tstart, last = (pt(E) for _ in range(4))
        when = pt(3 * (E - 1))
        due = U[:, 2 * CH:2 * CH + NCOL * 3 * (E - 1)]
        plan_f, eid_f = pt(NCOL + 1), pt(NCOL)

        PS = ctx.enter_context(nc.psum_tensor("PS", [P, 8 * 512], fp32))
        up_ps = PS[:, 0:2 * F]
        hT_ps = PS[:, 3 * 512:3 * 512 + HC * P]
        xT_ps = PS[:, 5 * 512:5 * 512 + D]
        y_ps = PS[:, 6 * 512:6 * 512 + D]
        tr_ps = PS[:, 7 * 512:8 * 512]
        xT0_ps = PS[:, 7 * 512:7 * 512 + D]
        xT1_ps = PS[:, 7 * 512 + D:7 * 512 + 2 * D]
        k_ps = PS[:, 0:2 * CH]
        yh_ps = PS[:, 2 * CH:4 * CH]
        cum_ps = PS[:, 4 * CH:6 * CH]
        rank_ps = PS[:, 6 * 512:6 * 512 + NT * E]
        tot_ps = PS[:, 6 * 512 + 128:6 * 512 + 128 + NT * E]
        table_ps = PS[:, 6 * 512 + 256:6 * 512 + 256 + NCOL]
        stat_ps = PS[:, 7 * 512:7 * 512 + 4]
        logit_ps = PS[:, 7 * 512:7 * 512 + NT * E]

        s_x = [sem(f"x_loaded{g}") for g in range(4)]
        s_small = sem("small_inputs_loaded")
        s_raw = sem("expert_loaded")
        s_const = sem("constants_made")
        s_dve = sem("dve_steps")
        s_xn = sem("xn_tile_pair_ready")
        s_xnd = sem("xn_stored")
        s_xtr = sem("xn_transposed")
        s_xnT = sem("xnT_ready")
        s_lg = sem("logits_done")
        s_mr = sem("group_scales_ready")
        s_pick = sem("picks_ready")
        s_rank = sem("ranks_done")
        s_pos = sem("onehots_ready")
        s_posu = sem("onehots_used")
        s_idx = sem("tables_ready")
        s_ctl = sem("tile_plan_ready")
        s_zin = sem("gap_ready")
        s_zex = sem("gap_exp_done")
        s_u0a = sem("u0_exp_done")
        s_u0b = sem("u0_logs_done")
        s_u0i = sem("u0_inputs_ready")
        s_nb = sem("minus_b_h_ready")
        s_kp = sem("k_projected")
        s_k = sem("k_and_h_projected")
        s_kb = sem("kb_ready")
        s_yr = sem("k_and_h_read")
        s_e = sem("act_chain")
        s_l1 = sem("l1_ready")
        s_l3 = sem("l3_ready")
        s_l2 = sem("l2_ready")
        s_c = sem("c_ready")
        s_cum = sem("cumsum_done")
        s_acp = sem("a_star_copied")
        s_u1 = sem("l3_minus_l2_ready")
        s_u2 = sem("k_minus_c_ready")
        s_u3 = sem("log_parts_summed")
        s_ua = sem("log_parts_complete")
        s_U = sem("u_ready")
        s_hi = sem("hi_pieces_ready")
        s_w = sem("expert_pieces_ready")
        s_gt = [sem(f"gathered{k}") for k in range(DEEP)]
        s_gc = sem("gather_column_ready")
        s_sc = sem("scatter_column_ready")
        s_rows = sem("rows_all_stored")
        s_xt = sem("x_tile_transposed")
        s_xhi = sem("x_hi_ready")
        s_xlo = sem("x_lo_ready")
        s_up = sem("up_done")
        s_silu = sem("silu_ready")
        s_g = sem("gated_ready")
        s_ht = sem("gated_transposed")
        s_hhi = sem("h_hi_ready")
        s_hlo = sem("h_lo_ready")
        s_dn = sem("down_done")
        s_y = sem("y_copied")
        s_st = [sem(f"scattered{k}") for k in range(DEEP)]
        s_M = sem("running_max_ready")
        s_D = sem("max_steps_ready")
        s_Em = sem("u_minus_max_ready")
        s_De = sem("decay_ready")
        s_Ee = sem("increment_ready")
        s_S = sem("scan_ready")
        s_lS = sem("log_scan_ready")
        s_L = sem("log_plus_max_ready")
        s_lh = sem("log_h_ready")
        s_mean_in = sem("sums_ready")
        s_mean = sem("mean_summed")
        s_var_in = sem("squares_ready")
        s_var = sem("squares_summed")
        s_norm = sem("norm_ready")
        s_xre = sem("x_loaded_again")
        s_hx = sem("h_exp_done")
        s_h = sem("h_ready")
        s_htr = sem("h_transposed")
        s_p1 = sem("stats_steps")
        s_p2 = sem("last_norm_steps")
        s_var0 = sem("group_variance_ready")
        s_std0 = sem("group_deviation_ready")
        s_std = sem("log_h_deviation_ready")
        s_std3 = sem("row_deviations_ready")
        s_yl = [[sem(f"y{k}_loaded{g}") for g in range(4)] for k in range(2)]
        s_fin = sem("result_ready")
        s_out = sem("result_stored")

        block = ctx.enter_context(nc.Block())

        def hold(eng, s, value):
            eng.wait_ge(s, value)
            eng.nop(nofuse=True)

        def tail(eng, tile, end=None):
            used = eng.value_load(tiles[0:1, 0:1], min_val=SURE, max_val=NTILES)
            for j in range(SURE, NTILES):
                with eng.If(used > j):
                    tile((j - 1) // LOOP, (j - 1) % LOOP)
                    eng.nop(nofuse=True)
            if end:
                for j in range(SURE, NTILES + 1):
                    with eng.If(used == j):
                        end(j)
                        eng.nop(nofuse=True)

        def chunk_of(v, c):
            return v[:, :].rearrange("p (q n) -> p q n", q=Q)[:, :, c * CH:(c + 1) * CH]

        def wslot(e, part, a):
            return wflat[:, ds(e % 2 * (2 * WALL) + (a + part * WALL), WP)]

        @block.sync
        def _(sp):
            for g in range(4):
                sp.dma_start(xn[:, 4 * g:4 * g + 4, :],
                             x[512 * g:512 * (g + 1), :].rearrange("(t p) d -> p t d", p=P)).then_inc(s_x[g], 16)
            for q in range(PIECES - 1):
                sp.dma_start(raw[:, q * WP:(q + 1) * WP], w_main[0][:, q * WP:(q + 1) * WP]).then_inc(s_raw, 16)
            sp.dma_start(raw[:, WP * (PIECES - 1):WMAIN], w_main[0][:, WP * (PIECES - 1):WMAIN]).then_inc(s_raw, 16)
            sp.dma_start(raw[P - TAIL:P, WMAIN:WALL], w_tail[0]).then_inc(s_raw, 16)
            for g in range(4):
                sp.wait_ge(s_xn, 2 * g + 2)
                sp.dma_start(xn_dram[512 * g:512 * (g + 1), :].rearrange("(t p) d -> p t d", p=P),
                             xn[:, 4 * g:4 * g + 4, :]).then_inc(s_xnd, 16)
            sp.wait_ge(s_U, NCH)
            with sp.Fori(1, E) as e:
                def row(w, a, b):
                    return w[ds(e, 1)][:, :, a:b].rearrange("a p n -> (a p) n")
                for q in range(PIECES):
                    sp.wait_ge(s_w, PIECES * e - (PIECES - 1) + q)
                    sp.dma_start(raw[:, q * WP:min((q + 1) * WP, WMAIN)],
                                 row(w_main, q * WP, min((q + 1) * WP, WMAIN))).then_inc(s_raw, 16)
                sp.dma_start(raw[P - TAIL:P, WMAIN:WALL], row(w_tail, 0, D)).then_inc(s_raw, 16)
            sp.wait_ge(s_rows, 1)
            for k, buf in ((0, U), (1, A)):
                for g in range(4):
                    sp.dma_start(buf[:, 1024 * g:1024 * (g + 1)].rearrange("p (t d) -> p t d", d=D),
                                 y_dram[k * NTOK + 512 * g:k * NTOK + 512 * (g + 1), :]
                                 .rearrange("(t p) d -> p t d", p=P)).then_inc(s_yl[k][g], 16)
            for g in range(4):
                sp.wait_ge(s_fin, g + 1)
                sp.dma_start(out[512 * g:512 * (g + 1), :].rearrange("(t p) d -> p t d", p=P),
                             xn[:, 4 * g:4 * g + 4, :]).then_inc(s_out, 16)
            sp.wait_ge(s_out, 64)

        @block.gpsimd
        def _(pool):
            pool.memset(ident[:, :], 0.0).then_inc(s_const, 1)
            pool.memset(ones[:, :], 1.0).then_inc(s_const, 1)
            pool.memset(tri[:, :], 1.0).then_inc(s_const, 1)
            pool.memset(ones_b[:, :], 1.0).then_inc(s_const, 1)
            pool.memset(tri_b[:, :], 1.0).then_inc(s_const, 1)
            pool.memset(raw[0:P - TAIL, WMAIN:WALL], 0.0).then_inc(s_const, 1)
            pool.wait_ge(s_const, 6)
            pool.affine_select(out=ident[:, :], in_=ident[:, :], compare_op=ALU.not_equal, fill=1.0, base=0,
                               pattern=[[-1, P]], channel_multiplier=1).then_inc(s_const, 1)
            pool.affine_select(out=tri[:, :], in_=tri[:, :], compare_op=ALU.is_ge, fill=0.0, base=0,
                               pattern=[[1, P]], channel_multiplier=-1).then_inc(s_const, 1)
            pool.affine_select(out=tri_b[:, :], in_=tri_b[:, :], compare_op=ALU.is_gt, fill=0.0, base=0,
                               pattern=[[1, P]], channel_multiplier=-1).then_inc(s_const, 1)
            pool.iota(iota_c[:, :], [[1, P]], base=0, channel_multiplier=0,
                      allow_small_or_imprecise_dtypes=True).then_inc(s_const, 1)
            pool.iota(id_f.rearrange("p (k t) -> p k t", k=2), [[NTOK, 2], [P, NT]], base=1, channel_multiplier=1,
                      allow_small_or_imprecise_dtypes=True).then_inc(s_const, 1)
            pool.iota(pad_row.rearrange("p (c u) -> p c u", u=DEEP), [[0, NCOL // DEEP], [P, DEEP]], base=SCRATCH + 1,
                      channel_multiplier=1, allow_small_or_imprecise_dtypes=True).then_inc(s_const, 1)
            pool.memset(eps[:, :], LN_EPS).then_inc(s_const, 1)
            pool.wait_ge(s_const, 13)
            for k in range(DEEP):
                pool.dma_start(y_dram[SCRATCH + (DEEP + k) * P:SCRATCH + (DEEP + k + 1) * P, 0:P],
                               ones[:, :]).then_inc(s_st[k], 16)
            for g in range(4):
                pool.wait_ge(s_mr, g + 1)
                for t in range(4 * g, 4 * g + 4):
                    ins = pool.tensor_scalar(xn[:, t, :], xn[:, t, :], rstd[:, t:t + 1], nmean[:, t:t + 1],
                                             ALU.mult, ALU.add)
                    if t % 2:
                        ins.then_inc(s_xn, 1)

            for q in range(PIECES):
                pool.wait_ge(s_hi, q + 1)
                lo, hi = (wbuf[:, 0, n, q * WP:(q + 1) * WP] for n in (1, 0))
                pool.tensor_tensor(lo, raw[:, q * WP:(q + 1) * WP], hi.bitcast(fp32), ALU.subtract).then_inc(s_w, 1)

            def h_logs(c):
                l3 = sets[c % 2][2]
                pool.wait_ge(s_l3, c + 1)
                pool.wait_ge(s_l2, c + 1)
                pool.tensor_tensor(l3, l3, l2s[c % 2], ALU.subtract).then_inc(s_u1, 1)

            def gate_logs(c):
                kb, l1, l3, _ = sets[c % 2]
                pool.wait_ge(s_c, c + 1)
                pool.tensor_tensor(kb, kb, l1, ALU.subtract).then_inc(s_u2, 1)
                h_logs(c)
                pool.wait_ge(s_u2, c + 1)
                pool.wait_ge(s_u1, c + 1)
                pool.tensor_tensor(kb, kb, l3, ALU.add).then_inc(s_u3, 1)
            gate_logs(0)
            gate_logs(1)
            gate_logs(2)
            pool.wait_ge(s_idx, 1)
            pool.wait_ge(s_xnd, 64)

            def gather(j, k):
                pool.tensor_copy(gcol[:, k:k + 1], gidx[:, ds(j, 1)]).then_inc(s_gc, 1)
                hold(pool, s_gc, j + 1)
                pool.indirect_dma_start(xg[:, k, :], None, xn_dram,
                                        bass.IndirectOffsetOnAxis(gcol[:, k:k + 1], 0)).then_inc(s_gt[k], 16)

            def scatter(j, k):
                pool.wait_ge(s_y, j + 2)
                pool.tensor_copy(scol[:, k:k + 1], sidx[:, ds(j, 1)]).then_inc(s_sc, 1)
                hold(pool, s_sc, j + 1)
                pool.indirect_dma_start(y_dram, bass.IndirectOffsetOnAxis(scol[:, k:k + 1], 0),
                                        ysb[:, k, :], None).then_inc(s_st[k], 16)

            def split_due(before, j):
                done = pool.value_load(plan[0:1, ds(j + 1, 1)], min_val=0, max_val=PIECES * (E - 1))
                with pool.If(before < done):
                    with pool.Fori(before, done) as p:
                        part = pool.snap(p % PIECES * WP)
                        hold(pool, s_hi, p + (PIECES + 1))
                        lo, hi = (wslot(p // PIECES + 1, n, part) for n in (1, 0))
                        pool.tensor_tensor(lo, raw[:, ds(part, WP)], hi.bitcast(fp32), ALU.subtract).then_inc(s_w, 1)
                return done

            for j in range(DEEP):
                gather(j, j)
            for r in range(2):
                g = ORDER[r]
                pool.wait_ge(s_M, r + 1)
                pool.tensor_tensor(Ug[:, g, :], Ug[:, g, :], M[:, g, :], ALU.subtract).then_inc(s_Em, 1)
                if r == 0:
                    h_logs(3)
            pool.wait_ge(s_xt, 1)
            gather(DEEP, 0)
            pool.wait_ge(s_ctl, 1)
            split_due(0, 0)

            def tile(i, u, done=None, hook=None):
                j = LOOP * i + (1 + u)
                if not isinstance(j, int) or j + DEEP < NTILES:
                    pool.wait_ge(s_xt, j + 1)
                    gather(j + DEEP, (1 + u) % DEEP)
                if hook:
                    hook(u)
                scatter(j - 1, u)
                if done is None:
                    done = pool.value_load(plan[0:1, ds(j, 1)], min_val=0, max_val=PIECES * (E - 1))
                return split_due(done, j)

            def body(i, hook=None):
                done = pool.value_load(plan[0:1, ds(LOOP * i + 1, 1)], min_val=0, max_val=PIECES * (E - 1))
                for u in range(LOOP):
                    done = tile(i, u, done, hook)

            def logh(r):
                g = ORDER[r]
                pool.wait_ge(s_L, r + 1)
                pool.tensor_tensor(Ag[:, g, :], Ug[:, g, :], Ag[:, g, :], ALU.subtract).then_inc(s_lh, 1)

            with pool.Fori(0, 2) as i:
                body(i)
            body(2, logh)
            with pool.Fori(3, 8) as i:
                body(i)

            def end(used):
                scatter(used - 1, (used - 1) % DEEP)
                for k in range(DEEP):
                    pool.wait_ge(s_gt[k], 16 * len(range(k, min(used + DEEP, NTILES), DEEP)))
                    pool.wait_ge(s_st[k], 16 * len(range(k, used, DEEP)) + 16)
                pool.sem_inc(s_rows, 1)
            tail(pool, tile, end)

        @block.scalar
        def _(act):
            act.dma_start(small_sb[:, :], small).then_inc(s_small, 16)
            act.wait_ge(s_const, 13)
            act.preload_act_table_set("sqrt_and_others")

            def deviations(g):
                act.wait_ge(s_var0, g + 1)
                act.activation(std[:, 4 * g:4 * g + 4], mv[:, 4 * g:4 * g + 4, 1], ACT.Sqrt,
                               bias=eps[:, :]).then_inc(s_std0, 1)

            def projected(c):
                kb, _, l3, nn = sets[c % 2]
                act.wait_ge(s_kp, c + 1)
                if c >= 2:
                    act.wait_ge(s_U, c - 1)
                if c == 1:
                    act.wait_ge(s_w, PIECES)
                for q in range(Q):
                    act.activation(kb[:, q * CH:(q + 1) * CH], k_ps[:, q * CH:(q + 1) * CH], ACT.Identity,
                                   bias=bias_sb[:, 0, q:q + 1]).then_inc(s_kb, 1)
                act.wait_ge(s_k, c + 1)
                for sign, dst, b in ((1.0, l3, bias_sb[:, 1, :]), (-1.0, nn, nbias[:, :])):
                    for q in range(Q):
                        act.activation(dst[:, q * CH:(q + 1) * CH], yh_ps[:, q * CH:(q + 1) * CH], ACT.Relu,
                                       scale=sign, bias=b[:, q:q + 1]).then_inc(s_yr, 1)

            def k_log(c):
                kb, l1, _, _ = sets[c % 2]
                act.wait_ge(s_kb, 2 * c + 2)
                act.activation(l1, kb, ACT.Abs).then_inc(s_e, 1)
                act.wait_ge(s_e, 3 * c + 1)
                act.activation(l1, l1, ACT.Exp, scale=-1.0).then_inc(s_e, 1)
                act.wait_ge(s_e, 3 * c + 2)
                act.activation(l1, l1, ACT.Ln, bias=1.0).then_inc(s_l1, 1)

            def h_logs(c):
                _, _, l3, nn = sets[c % 2]
                l2 = l2s[c % 2]
                act.wait_ge(s_yr, 4 * c + 4)
                if c >= 2:
                    act.wait_ge(s_u1, c - 1)
                act.activation(l2, nn, ACT.Exp, scale=-1.0).then_inc(s_e, 1)
                act.activation(l3, l3, ACT.Ln, scale=2.0, bias=1.0).then_inc(s_l3, 1)
                act.wait_ge(s_e, 3 * c + 3)
                act.activation(l2, l2, ACT.Ln, bias=1.0).then_inc(s_l2, 1)

            def evacuate(m):
                act.wait_ge(s_xtr, m + 1)
                act.activation(xnT[:, :, 2 * P * m:2 * P * (m + 1)].rearrange("p q (t n) -> p t q n", t=2),
                               PS[:, (4 + m % 2) * 512:(5 + m % 2) * 512].rearrange("p (t q n) -> p t q n", t=2, q=Q),
                               ACT.Copy).then_inc(s_xnT, 1)
            deviations(0)
            deviations(1)
            evacuate(0)
            deviations(2)
            evacuate(1)
            deviations(3)
            evacuate(2)
            evacuate(3)
            act.preload_act_table_set("natural_log_exp_and_others")
            act.wait_ge(s_nb, 1)
            projected(0)
            evacuate(4)
            evacuate(5)
            k_log(0)
            evacuate(6)
            evacuate(7)
            h_logs(0)
            act.wait_ge(s_u0i, 2)
            act.activation(u0t[:, 2, :], u0t[:, 0, :], ACT.Exp).then_inc(s_u0a, 1)
            act.activation(u0t[:, 3, :], u0t[:, 1, :], ACT.Ln, scale=2.0, bias=1.0).then_inc(s_u0b, 1)
            act.wait_ge(s_u0a, 1)
            act.activation(u0t[:, 4, :], u0t[:, 2, :], ACT.Ln, bias=1.0).then_inc(s_u0b, 1)

            def x_hi(j, slot, src=xT_ps):
                act.wait_ge(s_xt, j + 1)
                act.activation(xT[:, slot, 0, :], src, ACT.Copy).then_inc(s_xhi, 1)
            for c in range(1, NCH):
                projected(c)
                if c == NCH - 1:
                    x_hi(0, 0, xT0_ps)
                k_log(c)
                h_logs(c)
                if c == 1:
                    act.wait_ge(s_zin, 1)
                    act.activation(w12[:, 1, :], w12[:, 0, :], ACT.Exp).then_inc(s_zex, 1)

            def exps(r, between=None):
                g = ORDER[r]
                act.wait_ge(s_D, r + 1)
                act.activation(Dg[:, r, :], Dg[:, r, :], ACT.Exp).then_inc(s_De, 1)
                if between:
                    between()
                act.wait_ge(s_Em, r + 1)
                act.activation(Ug[:, g, :], Ug[:, g, :], ACT.Exp).then_inc(s_Ee, 1)

            def h_hi(j):
                act.wait_ge(s_ht, j + 1)
                act.wait_ge(s_dn, j)
                act.activation(hT[:, 0, :], hT_ps, ACT.Copy).then_inc(s_hhi, 1)

            def silu(j):
                act.wait_ge(s_up, j + 1)
                act.activation(sl, up_ps[:, 0:F], ACT.Silu).then_inc(s_silu, 1)

            def split_due(before, j):
                done = act.value_load(plan[0:1, ds(j + 1, 1)], min_val=0, max_val=PIECES * (E - 1))
                with act.If(before < done):
                    with act.Fori(before, done) as p:
                        part = act.snap(p % PIECES * WP)
                        hold(act, s_raw, p // PIECES * LOADS + 2 * LOADS)
                        act.activation(wslot(p // PIECES + 1, 0, part), raw[:, ds(part, WP)], ACT.Copy).then_inc(s_hi, 1)
                return done

            x_hi(1, 1, xT1_ps)
            exps(0)

            def last_a_copy():
                act.wait_ge(s_cum, NCH)
                act.activation(chunk_of(A, NCH - 1), cum_ps.rearrange("p (q n) -> p q n", q=Q),
                               ACT.Copy).then_inc(s_acp, 1)
            exps(1, last_a_copy)
            act.preload_act_table_set("silu_and_others")
            act.wait_ge(s_U, NCH - 1)
            silu(0)
            act.wait_ge(s_ht, 1)
            act.activation(hT[:, 0, :], hT_ps, ACT.Copy).then_inc(s_hhi, 1)
            act.wait_ge(s_ctl, 1)
            split_due(0, 0)

            def y_copy(j, u, value):
                act.wait_ge(s_dn, j + 1)
                act.wait_ge(s_st[u], value)
                act.activation(ysb[:, u, :], y_ps, ACT.Copy).then_inc(s_y, 1)

            def tile(i, u, done=None, hook=None, long=None):
                j = LOOP * i + (1 + u)
                silu(j)
                if long:
                    long()
                    if hook:
                        hook(u)
                    act.wait_ge(s_dn, j)
                else:
                    if not isinstance(j, int) or j < NTILES - 1:
                        x_hi(j + 1, u % 2)
                    if hook:
                        hook(u)
                    y_copy(j - 1, u, 16 * i + 16)
                    h_hi(j)
                if done is None:
                    done = act.value_load(plan[0:1, ds(j, 1)], min_val=0, max_val=PIECES * (E - 1))
                return split_due(done, j)

            def body(i, hook=None, long=None, at=None):
                done = act.value_load(plan[0:1, ds(LOOP * i + 1, 1)], min_val=0, max_val=PIECES * (E - 1))
                for u in range(LOOP):
                    done = tile(i, u, done, hook, long if u == at else None)

            def h_copy(i, m0):
                def run(u):
                    m = LOOP * i + (u - m0)
                    act.wait_ge(s_htr, m + 1)
                    act.activation(hst[:, :, :], A[:, :].rearrange("p (q n) -> p q n", q=Q)[:, :, ds(m * 2 * P, 2 * P)],
                                   ACT.Copy).then_inc(s_h, 1)
                return run

            def x_again(i, m0):
                def run(u):
                    m = LOOP * i + (u - m0)
                    act.wait_ge(s_p2, 4 * m + 1)
                    act.dma_start(xre, x[ds(m * 2 * P, 2 * P), :].rearrange("(t p) d -> p t d", p=P)
                                  ).then_inc(s_xre, 16)
                return run

            def second_exps():
                act.preload_act_table_set("natural_log_exp_and_others")
                exps(2)
                exps(3)
                act.preload_act_table_set("silu_and_others")

            def scan_logs():
                act.preload_act_table_set("natural_log_exp_and_others")
                for r in range(4):
                    g = ORDER[r]
                    act.wait_ge(s_S, r + 1)
                    act.activation(Ug[:, g, :], Ug[:, g, :], ACT.Ln).then_inc(s_lS, 1)
                act.preload_act_table_set("silu_and_others")

            def h_exps():
                act.wait_ge(s_var, 1)
                act.activation(gs[:, 15:16], stat_ps[:, 2:3], ACT.Sqrt, scale=1.0 / (NSTAT - 1)).then_inc(s_std, 1)
                act.preload_act_table_set("natural_log_exp_and_others")
                act.wait_ge(s_norm, 1)
                for g in range(4):
                    act.activation(Ag[:, g, :], Ag[:, g, :], ACT.Exp, scale=gs[:, 8:9],
                                   bias=gs[:, 9:10]).then_inc(s_hx, 1)
                act.preload_act_table_set("silu_and_others")

            def row_deviations():
                act.wait_ge(s_p1, 4 * NT // 2 + 1)
                act.activation(std[:, :], mv[:, :, 1], ACT.Sqrt, bias=eps[:, :]).then_inc(s_std3, 1)
                act.preload_act_table_set("silu_and_others")
            body(0)
            body(1, long=second_exps, at=0)
            body(2, long=scan_logs, at=0)
            body(3, long=h_exps, at=3)
            act.wait_ge(s_hx, 4)
            with act.Fori(4, 6) as i:
                body(i, hook=h_copy(i, LOOP * 4))
            body(6, hook=x_again(6, LOOP * 6), long=row_deviations, at=0)
            body(7, hook=x_again(7, LOOP * 6))
            tail(act, tile, lambda used: y_copy(used - 1, (used - 1) % DEEP, 16 * ((used - 1) // DEEP) + 16))

        @block.vector
        def _(dve):
            n = [0]

            def step(ins):
                n[0] += 1
                ins.then_inc(s_dve, 1)
                dve.wait_ge(s_dve, n[0])

            dve.sem_inc(s_y, 1)
            dve.sem_inc(s_htr, 1)
            dve.sem_inc(s_p1, 1)
            dve.sem_inc(s_p2, 1)
            dve.memset(one8, 1.0)
            dve.memset(keep.rearrange("p (e t) -> p e t", e=E)[:, :, 1:NT], 1.0)
            dve.memset(keep.rearrange("p (e t) -> p e t", e=E)[:, :, 0:1], 0.0)

            def stats(g):
                dve.wait_ge(s_x[g], 16)
                for t in range(4 * g, 4 * g + 4):
                    ins = dve.bn_stats(bst[:, t, :], xn[:, t, :])
                step(ins)
                for t in range(4 * g, 4 * g + 4):
                    ins = dve.bn_aggr(mv[:, t, :], bst[:, t, :])
                ins.then_inc(s_var0, 1)

            for g in range(4):
                stats(g)
                group = slice(4 * g, 4 * g + 4)
                dve.wait_ge(s_std0, g + 1)
                step(dve.reciprocal(rstd[:, group], std[:, group]))
                dve.scalar_tensor_tensor(nmean[:, group], mv[:, group, 0], -1.0, rstd[:, group], ALU.mult,
                                         ALU.mult).then_inc(s_mr, 1)
            dve.wait_ge(s_small, 16)
            dve.tensor_scalar(u0t[:, 0, :], h0_sb, 0.0, None, ALU.min).then_inc(s_u0i, 1)
            dve.tensor_scalar(u0t[:, 1, :], h0_sb, 0.0, None, ALU.max).then_inc(s_u0i, 1)
            dve.tensor_scalar(nbias[:, :], bias_sb[:, 1, :], -1.0, None, ALU.mult).then_inc(s_nb, 1)
            dve.wait_ge(s_raw, LOADS)
            for q in range(PIECES):
                dve.tensor_copy(wbuf[:, 0, 0, q * WP:(q + 1) * WP], raw[:, q * WP:(q + 1) * WP]).then_inc(s_hi, 1)

            def softplus(c):
                kb, l1, _, _ = sets[c % 2]
                dve.wait_ge(s_l1, c + 1)
                dve.wait_ge(s_kb, 2 * c + 2)
                dve.scalar_tensor_tensor(l1, kb, 0.0, l1, ALU.max, ALU.add).then_inc(s_c, 1)

            def parts(c):
                kb, _, _, nn = sets[c % 2]
                dve.wait_ge(s_u3, c + 1)
                dve.wait_ge(s_yr, 4 * c + 4)
                dve.tensor_tensor(kb, kb, nn, ALU.subtract).then_inc(s_ua, 1)

            def log_values(c):
                kb = sets[c % 2][0]
                dve.wait_ge(s_cum, c + 1)
                if c < NCH - 1:
                    dve.tensor_copy(chunk_of(A, c), cum_ps.rearrange("p (q n) -> p q n", q=Q)).then_inc(s_acp, 1)
                else:
                    dve.wait_ge(s_acp, NCH)
                dve.wait_ge(s_ua, c + 1)
                dve.tensor_tensor(chunk_of(U, c), kb.rearrange("p (q n) -> p q n", q=Q),
                                  cum_ps.rearrange("p (q n) -> p q n", q=Q), ALU.add).then_inc(s_U, 1)

            softplus(0)
            dve.wait_ge(s_lg, 1)

            def te(v):
                return v.rearrange("p (t e) -> p t e", e=E)

            def over_e(v):
                return v.rearrange("p (t a) -> p t a", a=1).to_broadcast([P, NT, E])
            ramp = iota_c[:, 0:E].rearrange("p (a e) -> p a e", a=1).to_broadcast([P, NT, E])
            step(dve.tensor_copy(logit, logit_ps))
            m1, m2 = m12[:, 0:NT], m12[:, NT:2 * NT]
            for mx, src, hot in ((m1, logit, hot1), (m2, t_b, hot2)):
                step(dve.tensor_reduce(mx, te(src), AX.X, ALU.max))
                step(dve.tensor_tensor(te(t_a), te(src), over_e(mx), ALU.is_equal))
                step(dve.scalar_tensor_tensor(te(t_a), ramp, float(P), te(t_a), ALU.subtract, ALU.mult))
                step(dve.tensor_reduce(idx8, te(t_a), AX.X, ALU.min))
                step(dve.scalar_tensor_tensor(te(hot), ramp, float(P), over_e(idx8), ALU.subtract, ALU.is_equal))
                if hot is hot1:
                    step(dve.scalar_tensor_tensor(t_b, hot1, -BIG, logit, ALU.mult, ALU.add))
            dve.tensor_tensor(w12[:, 0, :], m2, m1, ALU.subtract).then_inc(s_zin, 1)
            step(dve.tensor_tensor(pick, hot1, hot2, ALU.add))
            dve.tensor_copy(pick_b[:, :], pick).then_inc(s_pick, 1)
            dve.wait_ge(s_rank, 1)
            et = "p (e t) -> p e t"
            step(dve.tensor_copy(tot.rearrange(et, e=E), tot_ps.rearrange("p (t e) -> p e t", e=E)))
            step(dve.tensor_tensor_scan(cum, keep, tot, 0.0, ALU.mult, ALU.add))
            step(dve.tensor_copy(cnt, cum.rearrange(et, e=E)[:, :, NT - 1]))
            step(dve.tensor_scalar(eid_f[:, 0:NT], iota_c[:, 0:NT], float(P), None, ALU.mult))
            step(dve.tensor_tensor(thr.rearrange(et, e=E), cnt.rearrange("p (e a) -> p e a", a=1).to_broadcast([P, E, NT]),
                                   eid_f[:, 0:NT].rearrange("p (a t) -> p a t", a=1).to_broadcast([P, E, NT]), ALU.is_gt))
            step(dve.tensor_reduce(ntile, thr.rearrange(et, e=E), AX.X, ALU.add))
            step(dve.tensor_scalar(ntile, ntile, 1.0, None, ALU.max))
            step(dve.tensor_tensor_scan(tend, one8, ntile, 0.0, ALU.mult, ALU.add))
            step(dve.tensor_tensor(tstart, tend, ntile, ALU.subtract))
            step(dve.tensor_tensor(cum, cum, tot, ALU.subtract))
            step(dve.scalar_tensor_tensor(cum.rearrange(et, e=E), tstart.rearrange("p (e a) -> p e a", a=1)
                                          .to_broadcast([P, E, NT]), float(P), cum.rearrange(et, e=E), ALU.mult, ALU.add))
            step(dve.tensor_tensor(te(slots), cum.rearrange("p (e t) -> p t e", e=E), te(rank_ps), ALU.add))
            for k, hot in ((0, hot1), (1, hot2)):
                step(dve.tensor_tensor(t_a, hot, slots, ALU.mult))
                step(dve.tensor_reduce(slot_f[:, k * NT:(k + 1) * NT], te(t_a), AX.X, ALU.add))
            step(dve.tensor_copy(slot_i[:, 0, :], slot_f))
            step(dve.tensor_scalar(slot_i[:, 1, :], slot_i[:, 0, :], P - 1, None, ALU.bitwise_and))
            step(dve.tensor_scalar(slot_i[:, 2, :], slot_i[:, 0, :], 7, None, ALU.logical_shift_right))
            step(dve.tensor_copy(pos_f, slot_i[:, 1, :]))
            step(dve.tensor_copy(tile_f, slot_i[:, 2, :]))
            oh = onehot_tile.rearrange("p (s c) -> p s c", c=NCOL)
            step(dve.tensor_tensor(oh, iota_c[:, 0:NCOL].rearrange("p (a c) -> p a c", a=1).to_broadcast([P, 2 * NT, NCOL]),
                                   tile_f.rearrange("p (s a) -> p s a", a=1).to_broadcast([P, 2 * NT, NCOL]), ALU.is_equal))
            step(dve.tensor_tensor(oh, oh.bitcast(fp32), id_f.rearrange("p (s a) -> p s a", a=1)
                                   .to_broadcast([P, 2 * NT, NCOL]), ALU.mult))
            cols = iota_c[:, 0:NCOL].rearrange("p (c a) -> p c a", a=1)
            n_at = len(AT) - 1

            def tile_experts():
                c8 = cmp8.rearrange("p (c e) -> p c e", e=E)
                step(dve.tensor_tensor(c8, tend.rearrange("p (a e) -> p a e", a=1).to_broadcast([P, NCOL, E]),
                                       cols.to_broadcast([P, NCOL, E]), ALU.is_le))
                step(dve.tensor_reduce(eid_f, c8, AX.X, ALU.add))
                step(dve.tensor_scalar(eid_f, eid_f, float(E - 1), None, ALU.min))
                step(dve.tensor_copy(eid[:, :], eid_f))
                step(dve.tensor_scalar(last, tend, -1.0, None, ALU.add))
                step(dve.tensor_scalar(tiles[:, :], tend[:, E - 1:E], float(SURE), None, ALU.max))
                dve.memset(plan_f, 0.0)
                when3 = when.rearrange("p (a e) -> p a e", a=n_at)
                for k, at in enumerate(AT[1:]):
                    dve.tensor_scalar(when3[:, k, 1:], tstart[:, 1:E - 1], float(at), None, ALU.add)
                    ins = dve.tensor_scalar(when3[:, k, 0:1], tstart[:, 0:1], float(at + 1), None, ALU.add)
                step(ins)
                step(dve.tensor_tensor(when3, when3, last[:, 0:E - 1].rearrange("p (a e) -> p a e", a=1)
                                       .to_broadcast([P, n_at, E - 1]), ALU.min))

            def tile_plan():
                was = due.rearrange("p (c w) -> p c w", c=NCOL)
                step(dve.tensor_tensor(was, when.rearrange("p (a w) -> p a w", a=1)
                                       .to_broadcast([P, NCOL, n_at * (E - 1)]),
                                       cols.to_broadcast([P, NCOL, n_at * (E - 1)]), ALU.is_le))
                step(dve.tensor_reduce(plan_f[:, 1:NCOL + 1], was, AX.X, ALU.add))
                step(dve.tensor_reduce(eid_f, was[:, :, 0:E - 1], AX.X, ALU.add))
                step(dve.tensor_tensor(plan_f[:, 1:NCOL + 1], eid_f, plan_f[:, 1:NCOL + 1], ALU.add))
                dve.tensor_copy(plan[:, :], plan_f).then_inc(s_ctl, 1)
                dve.wait_ge(s_ctl, 1)

            for m in range(2 * NT // 4):
                if m == 2:
                    parts(0)
                    log_values(0)
                    softplus(1)
                    tile_experts()
                if m >= 2:
                    dve.wait_ge(s_posu, m - 1)
                dve.tensor_tensor(onehot_pos[:, m % 2, :].rearrange("p (s c) -> p s c", c=P),
                                  iota_c[:, :].rearrange("p (a c) -> p a c", a=1).to_broadcast([P, 4, P]),
                                  pos_f[:, 4 * m:4 * m + 4].rearrange("p (s a) -> p s a", a=1).to_broadcast([P, 4, P]),
                                  ALU.is_equal).then_inc(s_pos, 1)
            softplus(2)
            dve.wait_ge(s_posu, 2 * NT // 4)
            step(dve.tensor_copy(dtab, table_ps))
            step(dve.scalar_tensor_tensor(dpad, dtab, 0.0, pad_row, ALU.is_equal, ALU.mult))
            step(dve.tensor_scalar(dtab, dtab, -1.0, None, ALU.add))
            step(dve.tensor_scalar(dtok, dtab, float(NTOK), float(-NTOK), ALU.is_ge, ALU.mult))
            step(dve.tensor_tensor(dtok, dtok, dtab, ALU.add))
            step(dve.tensor_scalar(gidx[:, :], dtok, 0.0, None, ALU.max))
            step(dve.tensor_tensor(dpad, dpad, dtab, ALU.add))
            dve.tensor_copy(sidx[:, :], dpad).then_inc(s_idx, 1)
            dve.wait_ge(s_idx, 1)
            dve.wait_ge(s_zex, 1)
            step(dve.tensor_scalar(w12[:, 0, :], w12[:, 1, :], 1.0, None, ALU.add))
            step(dve.reciprocal(w12[:, 0, :], w12[:, 0, :]))
            step(dve.tensor_tensor(w12[:, 1, :], w12[:, 1, :], w12[:, 0, :], ALU.mult))
            dve.wait_ge(s_u0b, 2)
            step(dve.tensor_tensor(u0t[:, 5, :], u0t[:, 3, :], u0t[:, 4, :], ALU.subtract))
            for b in range(B):
                step(dve.tensor_tensor(u0[:, :].rearrange("p (q b) -> p q b", b=B)[:, :, b], u0t[:, 5, :],
                                       u0t[:, 0, :], ALU.add))

            def x_lo(j, slot, src=xT_ps):
                dve.wait_ge(s_xhi, j + 1)
                dve.tensor_tensor(xT[:, slot, 1, :], src, xT[:, slot, 0, :].bitcast(fp32),
                                  ALU.subtract).then_inc(s_xlo, 1)

            def h_lo(j):
                dve.wait_ge(s_hhi, j + 1)
                dve.tensor_tensor(hT[:, 1, :], hT_ps, hT[:, 0, :].bitcast(fp32), ALU.subtract).then_inc(s_hlo, 1)

            def gate(j):
                dve.wait_ge(s_silu, j + 1)
                dve.tensor_tensor(g_h, sl, up_ps[:, F:2 * F], ALU.mult).then_inc(s_g, 1)

            def run_max(r):
                g = ORDER[r]
                dve.tensor_tensor_scan(M[:, g, :], Ug[:, g, :], Ug[:, g, :], u0[:, g:g + 1],
                                       ALU.max, ALU.max).then_inc(s_M, 1)
                dve.wait_ge(s_M, r + 1)
                dve.tensor_tensor(Dg[:, r, 0:1], u0[:, g:g + 1], M[:, g, 0:1], ALU.subtract)
                dve.tensor_tensor(Dg[:, r, 1:T], M[:, g, 0:T - 1], M[:, g, 1:T], ALU.subtract).then_inc(s_D, 1)

            def less_max(r):
                g = ORDER[r]
                dve.tensor_tensor(Ug[:, g, :], Ug[:, g, :], M[:, g, :], ALU.subtract).then_inc(s_Em, 1)

            def run_scan(r):
                g = ORDER[r]
                dve.wait_ge(s_De, r + 1)
                dve.wait_ge(s_Ee, r + 1)
                dve.tensor_tensor_scan(Ug[:, g, :], Dg[:, r, :], Ug[:, g, :], 1.0, ALU.mult,
                                       ALU.add).then_inc(s_S, 1)

            def log_stats(r):
                g = ORDER[r]
                dve.wait_ge(s_lh, r + 1)
                for m in (2 * g, 2 * g + 1):
                    ins = dve.bn_stats(gst[:, m, :], A[:, 512 * m:512 * (m + 1)])
                return ins

            def plus_max(r):
                g = ORDER[r]
                dve.wait_ge(s_lS, r + 1)
                dve.tensor_tensor(Ug[:, g, :], Ug[:, g, :], M[:, g, :], ALU.add).then_inc(s_L, 1)
                if r:
                    log_stats(r - 1)
            parts(1)
            log_values(1)
            tile_plan()
            parts(2)
            x_lo(0, 0, xT0_ps)
            log_values(2)
            run_max(0)
            softplus(3)
            run_max(1)
            kb, l1, l3, _ = sets[(NCH - 1) % 2]
            dve.wait_ge(s_c, NCH)
            dve.tensor_tensor(kb, kb, l1, ALU.subtract).then_inc(s_u2, 1)
            dve.wait_ge(s_u1, NCH)
            dve.wait_ge(s_u2, NCH)
            dve.tensor_tensor(kb, kb, l3, ALU.add).then_inc(s_u3, 1)
            x_lo(1, 1, xT1_ps)
            parts(3)
            log_values(3)
            gate(0)
            h_lo(0)

            def tile(i, u, hook=None, relieve=False, first=None):
                j = LOOP * i + (1 + u)
                dve.wait_ge(s_ht, j)
                gate(j)
                if first:
                    first()
                if relieve:
                    dve.wait_ge(s_xt, j + 2)
                    dve.tensor_copy(xT[:, u % 2, 0, :], xT_ps).then_inc(s_xhi, 1)
                if not isinstance(j, int) or j < NTILES - 1:
                    x_lo(j + 1, u % 2)
                if relieve:
                    dve.wait_ge(s_dn, j)
                    dve.wait_ge(s_st[u], 16 * i + 16)
                    dve.tensor_copy(ysb[:, u, :], y_ps).then_inc(s_y, 1)
                    dve.wait_ge(s_ht, j + 1)
                    dve.tensor_copy(hT[:, 0, :], hT_ps).then_inc(s_hhi, 1)
                h_lo(j)
                if hook:
                    hook(u)

            def body(i, hook=None, relieve=None, first=None):
                for u in range(LOOP):
                    tile(i, u, hook, u == relieve, first if u == relieve else None)

            def sums():
                step(log_stats(3))
                step(dve.bn_aggr(gs[:, 0:2], gst[:, :, :].rearrange("p a b -> p (a b)")))
                step(dve.tensor_reduce(gs[:, 2:3], u0[:, :], AX.X, ALU.add))
                dve.scalar_tensor_tensor(gs[:, 3:4], gs[:, 0:1], float(2 * NTOK), gs[:, 2:3], ALU.mult,
                                         ALU.add).then_inc(s_mean_in, 1)

            def squares():
                dve.wait_ge(s_mean, 1)
                step(dve.tensor_scalar(gs[:, 4:5], stat_ps[:, 0:1], 1.0 / NSTAT, None, ALU.mult))
                step(dve.tensor_scalar(gs[:, 5:6], gs[:, 0:1], gs[:, 4:5], None, ALU.subtract))
                step(dve.scalar_tensor_tensor(gs[:, 6:7], gs[:, 5:6], gs[:, 5:6], gs[:, 1:2], ALU.mult, ALU.add))
                step(dve.tensor_scalar(gs[:, 10:14], u0[:, :], gs[:, 4:5], None, ALU.subtract))
                step(dve.tensor_tensor(gs[:, 10:14], gs[:, 10:14], gs[:, 10:14], ALU.mult))
                step(dve.tensor_reduce(gs[:, 14:15], gs[:, 10:14], AX.X, ALU.add))
                dve.scalar_tensor_tensor(gs[:, 7:8], gs[:, 6:7], float(2 * NTOK), gs[:, 14:15], ALU.mult,
                                         ALU.add).then_inc(s_var_in, 1)

            def normaliser():
                dve.wait_ge(s_std, 1)
                step(dve.reciprocal(gs[:, 8:9], gs[:, 15:16]))
                step(dve.scalar_tensor_tensor(gs[:, 9:10], gs[:, 4:5], -1.0, gs[:, 8:9], ALU.mult, ALU.mult))
                dve.sem_inc(s_norm, 1)

            def row_stats(i, m0):
                def run(u):
                    m = LOOP * i + (u - m0)
                    rows = xn[:, ds(2 * m, 2), :]
                    dve.wait_ge(s_htr, m + 2)
                    dve.tensor_tensor(rtmp, tr_ps.rearrange("p (t d) -> p t d", t=2), rows, ALU.add).then_inc(s_p1, 1)
                    hold(dve, s_p1, 4 * m + 2)
                    dve.tensor_copy(rows, rtmp)
                    for t in range(2):
                        ins = dve.bn_stats(st3[:, t, :], rtmp[:, t, :])
                    ins.then_inc(s_p1, 1)
                    hold(dve, s_p1, 4 * m + 3)
                    for t in range(2):
                        ins = dve.bn_aggr(mv3[:, t, :], st3[:, t, :])
                    ins.then_inc(s_p1, 1)
                    dve.wait_ge(s_p1, 4 * m + 4)
                    dve.tensor_copy(mv[:, ds(2 * m, 2), :], mv3[:, :, :]).then_inc(s_p1, 1)
                return run

            def last_norm(i, m0):
                def run(u):
                    m = LOOP * i + (u - m0)
                    rows = xn[:, ds(2 * m, 2), :]
                    for t in range(2):
                        row = xn[:, ds(2 * m + t, 1), :].rearrange("p a d -> p (a d)")
                        ins = dve.tensor_scalar(row, row, mv[:, ds(2 * m + t, 1), 0:1].rearrange("p a b -> p (a b)"),
                                                rstd[:, ds(2 * m + t, 1)], ALU.subtract, ALU.mult)
                    ins.then_inc(s_p2, 1)
                    dve.wait_ge(s_p2, 4 * m + 2)
                    for k in range(2):
                        dve.tensor_tensor(rows, rows, lnwb[:, k:k + 1, :].to_broadcast([P, 2, D]),
                                          ALU.add if k else ALU.mult).then_inc(s_p2, 1)
                        dve.wait_ge(s_p2, 4 * m + (3 + k))
                    dve.wait_ge(s_xre, 16 * m + 16)
                    dve.tensor_tensor(rows, rows, xre, ALU.add).then_inc(s_p2, 1)
                return run

            def global_stats(u):
                if u < 2:
                    (sums, squares)[u]()

            def second_max(u):
                (run_max, less_max)[u // 2](2 + u % 2)

            def row_scales():
                dve.wait_ge(s_std3, 1)
                step(dve.reciprocal(rstd[:, :], std[:, :]))

            body(0, second_max)
            body(1, run_scan, relieve=0)
            body(2, plus_max, relieve=0)
            body(3, global_stats, relieve=3, first=normaliser)
            with dve.Fori(4, 6) as i:
                body(i, row_stats(i, LOOP * 4))
            body(6, last_norm(6, LOOP * 6), relieve=0, first=row_scales)
            body(7, last_norm(7, LOOP * 6))
            tail(dve, tile)
            for k, buf in ((0, U), (1, A)):
                for g in range(4):
                    dve.wait_ge(s_yl[k][g], 16)
                    for t in range(4 * g, 4 * g + 4):
                        ins = dve.scalar_tensor_tensor(xn[:, t, :], buf[:, D * t:D * (t + 1)], w12[:, k, t:t + 1],
                                                       xn[:, t, :], ALU.mult, ALU.add)
                    if k:
                        ins.then_inc(s_fin, 1)
                if k == 0:
                    step(ins)

        @block.tensor
        def _(pe):
            pe.wait_ge(s_const, 13)
            pe.wait_ge(s_small, 16)

            def project(c):
                for mat, base in ((0, 0), (1, 2 * CH)):
                    if c and mat == 0:
                        pe.wait_ge(s_kb, 2 * c)
                    if c and mat == 1:
                        pe.wait_ge(s_yr, 4 * c)
                    for qo in range(Q):
                        for q in range(Q):
                            ins = pe.matmul(PS[:, base + qo * CH:base + (qo + 1) * CH],
                                            wzh_sb[:, q, mat, qo * P:(qo + 1) * P], xnT[:, q, c * CH:(c + 1) * CH],
                                            start=(q == 0), stop=(q == Q - 1))
                    ins.then_inc(s_k if mat else s_kp, 1)

            def cumsum(c):
                pe.wait_ge(s_c, c + 1)
                l1 = sets[c % 2][1]
                if c:
                    pe.wait_ge(s_U, c)
                pe.matmul(cum_ps[:, 0:CH], tri[:, :], l1[:, 0:CH], start=True, stop=True)
                pe.matmul(cum_ps[:, CH:2 * CH], ones[:, :], l1[:, 0:CH], start=True, stop=False)
                pe.matmul(cum_ps[:, CH:2 * CH], tri[:, :], l1[:, CH:2 * CH], start=False,
                          stop=True).then_inc(s_cum, 1)

            for m in range(NT // 2):
                pe.wait_ge(s_xn, m + 1)
                if m >= 2:
                    pe.wait_ge(s_xnT, m - 1)
                for t in range(2):
                    for q in range(Q):
                        col = (4 + m % 2) * 512 + (t * Q + q) * P
                        ins = pe.transpose(PS[:, col:col + P], xn[:, 2 * m + t, q * P:(q + 1) * P], ident[:, :])
                ins.then_inc(s_xtr, 1)
                for k in (m - 1, m) if m == NT // 2 - 1 else (m - 1,) if m else ():
                    pe.wait_ge(s_xnT, k + 1)
                    for t in (2 * k, 2 * k + 1):
                        for q in range(Q):
                            ins = pe.matmul(logit_ps[:, t * E:(t + 1) * E], xnT[:, q, t * P:(t + 1) * P],
                                            wg_sb[:, q, :], start=(q == 0), stop=(q == Q - 1))
                if m == 3:
                    project(0)
            ins.then_inc(s_lg, 1)

            def ranks():
                pe.wait_ge(s_pick, 1)
                pe.matmul(rank_ps, tri_b[:, :], pick_b[:, :], start=True, stop=True)
                pe.matmul(tot_ps, ones_b[:, :], pick_b[:, :], start=True, stop=True).then_inc(s_rank, 1)
            cumsum(0)
            ranks()
            project(1)
            project(2)
            cumsum(1)
            for m in range(2 * NT // 4):
                pe.wait_ge(s_pos, m + 1)
                for s in range(4):
                    r = 4 * m + s
                    ins = pe.matmul(table_ps, onehot_pos[:, m % 2, s * P:(s + 1) * P],
                                    onehot_tile[:, r * NCOL:(r + 1) * NCOL], start=(r == 0), stop=(r == 2 * NT - 1))
                ins.then_inc(s_posu, 1)
            project(3)

            def x_tile(j, k, val, dst=xT_ps):
                pe.wait_ge(s_gt[k], val)
                for q in range(Q):
                    ins = pe.transpose(dst[:, q * P:(q + 1) * P], xg[:, k, q * P:(q + 1) * P], ident[:, :])
                ins.then_inc(s_xt, 1)
            cumsum(2)
            x_tile(0, 0, 16, xT0_ps)

            def either(e, products):
                if isinstance(e, int):
                    products(e % 2)
                    return
                with pe.If(e % 2 > 0):
                    products(1)
                with pe.Else():
                    products(0)

            def up(j, slot, e):
                pe.wait_ge(s_xlo, j + 1)
                hold(pe, s_w, PIECES * e + (PIECES - 1))

                def products(w):
                    for q in range(Q):
                        for xpart, wpart in ((0, 0), (0, 1), (1, 0)):
                            for a, b in UP_PIECES:
                                ins = pe.matmul(up_ps[:, a:b], xT[:, slot, xpart, q * P:(q + 1) * P],
                                                wbuf[:, w, wpart, q * 2 * F + a:q * 2 * F + b],
                                                start=(q == 0 and xpart == 0 and wpart == 0),
                                                stop=(q == Q - 1 and xpart == 1))
                    ins.then_inc(s_up, 1)
                either(e, products)

            def down(j, e):
                pe.wait_ge(s_w, PIECES * e + PIECES)
                pe.wait_ge(s_y, j + 1)
                hold(pe, s_hlo, j + 1)

                def products(w):
                    for c in range(HC):
                        for hpart, wpart in ((0, 0), (0, 1), (1, 0)):
                            ins = pe.matmul(y_ps, hT[:, hpart, c * P:(c + 1) * P],
                                            wbuf[:, w, wpart, W13 + c * D:W13 + (c + 1) * D],
                                            start=(c == 0 and hpart == 0 and wpart == 0),
                                            stop=(c == HC - 1 and hpart == 1))
                    ins.then_inc(s_dn, 1)
                either(e, products)

            def h_tile(j):
                pe.wait_ge(s_g, j + 1)
                for c in range(HC):
                    a = min(c * P, F - P)
                    ins = pe.transpose(hT_ps[:, c * P:(c + 1) * P], g_h[:, a:a + P], ident[:, :])
                ins.then_inc(s_ht, 1)

            pe.wait_ge(s_kb, 2 * NCH)
            pe.wait_ge(s_yr, 4 * NCH)
            up(0, 0, 0)
            x_tile(1, 1, 16, xT1_ps)
            cumsum(3)
            pe.wait_ge(s_U, NCH)
            h_tile(0)
            pe.wait_ge(s_ctl, 1)

            def expert(j):
                return pe.value_load(eid[0:1, ds(j, 1)], min_val=0, max_val=E - 1)

            r_before, r_e = pe.alloc_register("expert_before"), pe.alloc_register("expert")
            pe.reg_mov(r_before, 0)
            pe.reg_mov(r_e, expert(1))

            def tile(i, u, hook=None):
                j = LOOP * i + (1 + u)
                before, e = (pe.snap(r, min_val=0, max_val=E - 1) for r in (r_before, r_e))
                pe.wait_ge(s_g, j)
                up(j, (1 + u) % 2, e)
                if not isinstance(j, int) or j < NTILES - 1:
                    x_tile(j + 1, (2 + u) % DEEP, 16 * i + 16 * ((2 + u) // DEEP + 1))
                down(j - 1, before)
                pe.reg_mov(r_before, e)
                pe.reg_mov(r_e, expert(j + 1))
                h_tile(j)
                if hook:
                    hook(u)

            def body(i, hook=None):
                for u in range(LOOP):
                    tile(i, u, hook)

            def sum_all(src, col, s_in, s_out):
                pe.wait_ge(s_in, 1)
                pe.matmul(stat_ps[:, col:col + 1], ones[:, :], src, start=True, stop=True).then_inc(s_out, 1)

            def h_back(i, m0):
                def run(u):
                    m = LOOP * i + (u - m0)
                    pe.wait_ge(s_h, m + 1)
                    pe.wait_ge(s_p1, 4 * m + 1)
                    for t in range(2):
                        for q in range(Q):
                            col = (t * Q + q) * P
                            ins = pe.transpose(tr_ps[:, col:col + P], hst[:, q, t * P:(t + 1) * P], ident[:, :])
                    ins.then_inc(s_htr, 1)
                return run

            def global_stats(u):
                if u == 1:
                    sum_all(gs[:, 3:4], 0, s_mean_in, s_mean)
                if u == 2:
                    sum_all(gs[:, 7:8], 2, s_var_in, s_var)
            with pe.Fori(0, 3) as i:
                body(i)
            body(3, hook=global_stats)
            with pe.Fori(4, 6) as i:
                body(i, hook=h_back(i, LOOP * 4))
            with pe.Fori(6, 8) as i:
                body(i)
            tail(pe, tile, lambda used: down(used - 1, pe.snap(r_before, min_val=0, max_val=E - 1)))


def kernel(**inputs):
    import numpy as _np
    import concourse.bacc as _bacc
    from concourse import mybir as _mybir
    from concourse.bass_utils import run_bass_kernel_spmd as _run

    a = {k: _np.ascontiguousarray(v) for k, v in inputs.items()}
    w1, w2, w3 = a["L0_ffn_w1"], a["L0_ffn_w2"], a["L0_ffn_w3"]
    up = _np.concatenate([w1, w3], 1).transpose(0, 2, 1).reshape(E, Q, P, 2 * F).transpose(0, 2, 1, 3)
    dn = w2.transpose(0, 2, 1)
    main = _np.concatenate([up.reshape(E, P, W13),
                            dn[:, 0:FULL * P].reshape(E, FULL, P, D).transpose(0, 2, 1, 3).reshape(E, P, FULL * D)], 2)
    zh = _np.stack([a["L0_attn_W_z"].T, a["L0_attn_W_h"].T], 1)
    small = {
        "wzh": zh.reshape(Q, P, 2, D).transpose(1, 0, 2, 3),
        "wg": a["L0_ffn_w_gate"].T.reshape(Q, P, E).transpose(1, 0, 2),
        "bias": _np.stack([a["L0_attn_b_z"], a["L0_attn_b_h"]]).reshape(2, Q, P).transpose(2, 0, 1),
        "h0": a["L0_attn_h0"].reshape(Q, P).T,
        "ln": _np.stack([a["L0_attn_ln_w"], a["L0_attn_ln_b"]])[None].repeat(P, 0),
    }
    arrays = {
        "x": a["L0_attn_hidden_states"].reshape(NTOK, D),
        "small": _np.concatenate([small[name].reshape(P, n) for name, n in SMALL], 1),
        "w_main": main,
        "w_tail": dn[:, FULL * P:],
    }
    arrays = {k: _np.ascontiguousarray(v) for k, v in arrays.items()}
    nc = _bacc.Bacc("TRN2", target_bir_lowering=False, num_devices=1)
    f32 = _mybir.dt.float32
    args = [nc.dram_tensor(n, v.shape, f32, kind="ExternalInput").ap() for n, v in arrays.items()]
    args.append(nc.dram_tensor("out", [NTOK, D], f32, kind="ExternalOutput").ap())
    args.append(nc.dram_tensor("xn_dram", [NTOK, D], f32).ap())
    args.append(nc.dram_tensor("y_dram", [2 * NTOK + 2 * DEEP * P, D], f32).ap())
    build_program(nc, *args)
    r = _run(nc, [arrays], core_ids=[0])
    return r.results[0]["out"].reshape(B, T, D)
```
